# Optimizing a Trainium2 kernel written in Bass

```python
import numpy as np
import jax
import jax.numpy as jnp

def _softmax(x, axis=-1):
    return jax.nn.softmax(x, axis=axis)

def _gelu(x):
    return jax.nn.gelu(x, approximate=True)

def _silu(x):
    return jax.nn.silu(x)

def _sigmoid(x):
    return jax.nn.sigmoid(x)

def _layernorm(x, axis=-1, eps=1e-05):
    m = jnp.mean(x, axis=axis, keepdims=True)
    v = jnp.var(x, axis=axis, keepdims=True)
    return (x - m) / jnp.sqrt(v + eps)

def _scatter_add(tgt, idx, src, axis=0):
    return tgt.at[idx].add(src)

def _segment_sum(src, seg, n):
    return jax.ops.segment_sum(src, seg, n)
kernel_name = 'mk_gnn_resnorm_d1_gnn_r8_0db782'

def setup_inputs(seed: int=0):
    np.random.seed(seed)
    _w = jnp.asarray

    def _rec_inputs():
        import jax
        import jax.numpy as jnp
        _gk = jax.random.key(seed)
        x = -0.0001006 + 1 * jax.random.normal(jax.random.fold_in(_gk, 1), (6250, 96), jnp.float32)
        src = jax.random.randint(jax.random.fold_in(_gk, 2), (100000,), 0, 6250, jnp.int32)
        dst = jax.random.randint(jax.random.fold_in(_gk, 3), (100000,), 0, 6250, jnp.int32)
        _o = jnp.argsort(dst, stable=True)
        src = src[_o]
        dst = dst[_o]
        edge_attr_96 = 5.93493e-05 + 1.00006 * jax.random.normal(jax.random.fold_in(_gk, 11), (100000, 96), jnp.float32)
        return (x, src, dst, edge_attr_96)
    x, src, dst, edge_attr_96 = _rec_inputs()

    def _L0_gnn_setup():
        import jax, jax.numpy as jnp
        import numpy as np
        N_NODES = 6250
        N_EDGES = 100000
        IN_DIM = 96
        NUM_HEADS = 8
        HEAD_DIM = IN_DIM // NUM_HEADS
        key = jax.random.key(seed)
        ks = jax.random.split(key, 11)
        s = 1.0 / np.sqrt(IN_DIM)
        return {'x': jax.random.normal(ks[0], (N_NODES, IN_DIM), dtype=jnp.float32), 'edge_index': jax.random.randint(ks[1], (2, N_EDGES), 0, N_NODES, dtype=jnp.int64), 'edge_attr': jax.random.normal(ks[2], (N_EDGES, IN_DIM), dtype=jnp.float32), 'Wq': jax.random.normal(ks[3], (IN_DIM, IN_DIM), dtype=jnp.float32) * s, 'bq': jax.random.normal(ks[4], (IN_DIM,), dtype=jnp.float32) * s, 'Wk': jax.random.normal(ks[5], (IN_DIM, IN_DIM), dtype=jnp.float32) * s, 'bk': jax.random.normal(ks[6], (IN_DIM,), dtype=jnp.float32) * s, 'We': jax.random.normal(ks[7], (IN_DIM, IN_DIM), dtype=jnp.float32) * s, 'be': jax.random.normal(ks[8], (IN_DIM,), dtype=jnp.float32) * s, 'Wv': jax.random.normal(ks[9], (IN_DIM, IN_DIM), dtype=jnp.float32) * s, 'bv': jax.random.normal(ks[10], (IN_DIM,), dtype=jnp.float32) * s}
    _L0_gnn_all = _L0_gnn_setup()
    _L0_gnn_in = {k: v for k, v in _L0_gnn_all.items() if k in ('Wq', 'bq', 'Wk', 'bk', 'We', 'be', 'Wv', 'bv')}
    del _L0_gnn_all
    return {'x': x, 'src': src, 'dst': dst, 'edge_attr_96': edge_attr_96, 'L0_gnn_Wq': _L0_gnn_in['Wq'], 'L0_gnn_bq': _L0_gnn_in['bq'], 'L0_gnn_Wk': _L0_gnn_in['Wk'], 'L0_gnn_bk': _L0_gnn_in['bk'], 'L0_gnn_We': _L0_gnn_in['We'], 'L0_gnn_be': _L0_gnn_in['be'], 'L0_gnn_Wv': _L0_gnn_in['Wv'], 'L0_gnn_bv': _L0_gnn_in['bv']}

def reference(x, src, dst, edge_attr_96, L0_gnn_Wq, L0_gnn_bq, L0_gnn_Wk, L0_gnn_bk, L0_gnn_We, L0_gnn_be, L0_gnn_Wv, L0_gnn_bv):
    import jax
    import jax.numpy as jnp

    def _L0_gnn_ref(x, edge_index, edge_attr, Wq, bq, Wk, bk, We, be, Wv, bv):
        import jax, jax.numpy as jnp
        import numpy as np
        N_NODES = 6250
        N_EDGES = 100000
        IN_DIM = 96
        NUM_HEADS = 8
        HEAD_DIM = IN_DIM // NUM_HEADS
        N = x.shape[0]
        H, D = (NUM_HEADS, HEAD_DIM)
        Q_h = (x @ Wq + bq).reshape(N, H, D)
        K_h = (x @ Wk + bk).reshape(N, H, D)
        V_h = (x @ Wv + bv).reshape(N, H, D)
        E = (edge_attr @ We + be).reshape(-1, H, D)
        src_idx = edge_index[0]
        dst_idx = edge_index[1]
        src = K_h[src_idx]
        dest = Q_h[dst_idx]
        score = src * dest / jnp.sqrt(jnp.asarray(D, x.dtype))
        score = score * E
        score = jnp.exp(jnp.clip(score.sum(-1, keepdims=True), -5.0, 5.0))
        msg = V_h[src_idx] * score
        wV = jax.ops.segment_sum(msg, dst_idx, num_segments=N)
        Z = jax.ops.segment_sum(score, dst_idx, num_segments=N)
        h_out = wV / (Z + 1e-06)
        return h_out.reshape(N, H * D)
    edge_index = jnp.stack([src, dst])
    x = _layernorm(x + _L0_gnn_ref(x, edge_index, edge_attr_96, L0_gnn_Wq, L0_gnn_bq, L0_gnn_Wk, L0_gnn_bk, L0_gnn_We, L0_gnn_be, L0_gnn_Wv, L0_gnn_bv), axis=-1)
    return x

_drawn_inputs = setup_inputs


def setup_inputs(seed=0):
    import zlib

    import numpy as np

    out = dict(_drawn_inputs(seed))
    spreads = {}
    factors = {}
    for name, (base, spread) in spreads.items():
        noise = np.random.default_rng([zlib.crc32(name.encode()), seed]).standard_normal(out[name].shape)
        drawn = base * np.exp(spread * noise) if base else spread * noise
        out[name] = jnp.asarray(drawn.astype(out[name].dtype))
    for name, factor in factors.items():
        out[name] = (out[name] * factor).astype(out[name].dtype)
    return out
```

```python
import concourse.bass as bass
from concourse import mybir
from contextlib import ExitStack

P = 128
N = 6250
E = 100000
D = 96
H = 8
HD = D // H
DA = D + 1
T = 8
GE = T * P
NG = -(-E // GE)
LAST_TILES = -(-E // P) - (NG - 1) * T
NW = -(-N // P)
NR = (NW + 1) * P
ML = D + H
EPS_Z = 1e-6
EPS_LN = 1e-5
U = 4
TURNS = (NG - 4) // U
NCH = 5
CT = NR // P // NCH
OT = NW


def lap(r, k, ring):
    return (U // ring) * r + k // ring + 1


def gnn_program(nc, xT, xrows, src, dst_group, dst_tile, eaT, w_node, w_edge, out):
    f32, bf16, i32 = mybir.dt.float32, mybir.dt.bfloat16, mybir.dt.int32
    ALU, ACT, AX = mybir.AluOpType, mybir.ActivationFunctionType, mybir.AxisListType

    kv_table = nc.dram_tensor("kv_table", (NR, 2 * D), f32, kind="Internal").ap()
    q_table = nc.dram_tensor("q_table", (NR, 3 * D), bf16, kind="Internal").ap()
    rel_table = nc.dram_tensor("rel_table", (NG, GE), bf16, kind="Internal").ap()
    range_table = nc.dram_tensor("range_table", (NG, 2), f32, kind="Internal").ap()
    acc_table = nc.dram_tensor("acc_table", (NR, ML), f32, kind="Internal").ap()

    ctx = ExitStack()
    with ctx:
        def sb(name, shape, dt):
            return ctx.enter_context(nc.sbuf_tensor(name, shape, dt))

        def ps(name, shape, dt):
            return ctx.enter_context(nc.psum_tensor(name, shape, dt))

        sems = []

        def sem(name):
            sems.append(ctx.enter_context(nc.semaphore(name)))
            return sems[-1]

        wn = sb("wn", [DA, 3 * D], f32)
        we = sb("we", [DA, D], f32)
        xt = sb("xt", [P, NR], f32)
        kv_stage = sb("kv_stage", [P, 2, CT, 2 * D], f32)
        q_parts = sb("q_parts", [P, 2, CT, 3, D], bf16)
        q_rest = sb("q_rest", [P, 2, 2, D], f32)
        zeros = sb("zeros", [P, NR // P * ML], f32)
        dstg = sb("dstg", [NG, GE], i32)
        dstp = sb("dstp", [P, NG * T], i32)
        dst_masked = sb("dst_masked", [NG, GE], f32)
        ranges = sb("ranges", [NG, 4], f32)
        ranges_all = sb("ranges_all", [P, NG, 2], f32)
        fits = sb("fits", [P, 2], f32)
        base_all = sb("base_all", [P, NG], f32)
        base_int = sb("base_int", [P, NG], i32)
        flag_int = sb("flag_int", [P, 1], i32)
        window = sb("window", [P, 1], f32)
        rel_group = sb("rel_group", [NG, GE], bf16)
        rel_tile = sb("rel_tile", [P, NG * T], bf16)
        node_id = sb("node_id", [P, 1], f32)
        node_row = sb("node_row", [P, P], f32)
        idx = sb("idx", [P, 4, T], i32)
        kv = sb("kv", [P, 4, T, 2 * D], f32)
        ea = sb("ea", [DA, 2, GE], f32)
        rel = sb("rel", [P, 2, GE], bf16)
        qwin = sb("qwin", [P, 2, 3, D], bf16)
        pick = sb("pick", [P, 2, GE], bf16)
        place = sb("place", [P, 2, T, P], f32)
        qk = sb("qk", [P, T, D], f32)
        qke = sb("qke", [P, T, D], f32)
        logit = sb("logit", [P, T * H], f32)
        clipped = sb("clipped", [P, 2, T * H], f32)
        msg = sb("msg", [P, 2, T, ML], f32)
        accw = sb("accw", [P, 2, ML], f32)
        psE = ps("psE", [P, 2, 512], f32)
        psQ = ps("psQ", [P, 2, 512], f32)
        psA = ps("psA", [P, 2, 512], f32)
        psI = ps("psI", [P, 512], f32)
        psW = ps("psW", [P, 512], f32)
        ps_ids = psI[:, 0:P]
        ps_wt = psW[:, 0:T * H]
        kv_banks = [psE[:, 0], psE[:, 1], psA[:, 0], psA[:, 1]]

        w_in, we_in, dst_in = sem("w_in"), sem("we_in"), sem("dst_in")
        xt_in = [sem(f"xt_in{c}") for c in range(NCH)]
        ones_set, ids_made, ids_up, zero_set = sem("ones_set"), sem("ids_made"), sem("ids_up"), sem("zero_set")
        kv_mm, kv_up = sem("kv_mm"), sem("kv_up")
        kv_out = [sem("kv_out0"), sem("kv_out1")]
        q_mm, q_hi, q_r, q_mid, q_up = sem("q_mm"), sem("q_hi"), sem("q_r"), sem("q_mid"), sem("q_up")
        q_out = [sem("q_out0"), sem("q_out1")]
        acc_zeroed = sem("acc_zeroed")
        range_up, range_out, range_in = sem("range_up"), sem("range_out"), sem("range_in")
        tables_chain, tables_up, rel_out = sem("tables_chain"), sem("tables_up"), sem("rel_out")

        idx_in = [sem(f"idx_in{i}") for i in range(4)]
        kv_in = [sem(f"kv_in{i}") for i in range(4)]
        ea_in = [sem(f"ea_in{i}") for i in range(2)]
        rel_in = [sem(f"rel_in{i}") for i in range(2)]
        qwin_in = [sem(f"qwin_in{i}") for i in range(2)]
        accw_in = [sem(f"accw_in{i}") for i in range(2)]
        accw_out = [sem(f"accw_out{i}") for i in range(2)]
        e_done, q_done, sum_done = sem("e_done"), sem("q_done"), sem("sum_done")
        pick_done, place_done, qk_done, qke_done = sem("pick_done"), sem("place_done"), sem("qk_done"), sem("qke_done")
        logit_done, clip_done, msg_done, merge_done = sem("logit_done"), sem("clip_done"), sem("msg_done"), sem("merge_done")
        exp_done, wt_done = sem("exp_done"), sem("wt_done")
        gathers_begun = sem("gathers_begun")
        epi = [sem(f"epi{i}") for i in range(12)]

        def engine_turns(eng, body):
            for k in range(U):
                body(0, k, k)
            with eng.Fori(1, TURNS) as r:
                for k in range(U):
                    body(r, k, U + k)
            for at in range(TURNS * U, NG + 2):
                body(TURNS, at - TURNS * U, at)

        def edge_pass(first):
            block = nc.Block()
            with block as block:

                @block.sync
                def _(sp):
                    if first:
                        sp.dma_start(wn[:], w_node).then_inc(w_in, 16)
                        for c in range(NCH):
                            cols = slice(c * CT * P, (c + 1) * CT * P)
                            sp.dma_start(xt[0:D, cols], xT[:, cols]).then_inc(xt_in[c], 16)
                            if c == 0:
                                sp.dma_start(dstg[:], dst_group).then_inc(dst_in, 16)
                                sp.dma_start(dstp[:], dst_tile).then_inc(dst_in, 16)
                        sp.dma_start(we[:], w_edge).then_inc(we_in, 16)
                        sp.wait_ge(range_up, 1)
                        sp.dma_start(range_table, ranges[:, 0:2]).then_inc(range_out, 16)
                        sp.wait_ge(range_out, 16)
                        sp.dma_start(ranges_all[:].rearrange("p g c -> p (g c)"),
                                     range_table.rearrange("g c -> (g c)").unsqueeze(0).broadcast_to([P, NG * 2])
                                     ).then_inc(range_in, 16)
                    sp.wait_ge(tables_up, 1)
                    sp.dma_start(rel_table, rel_group[:]).then_inc(rel_out, 16)
                    if first:
                        kv_ = kv_table.rearrange("(c t p) f -> c p t f", t=CT, p=P)
                        q_ = q_table.rearrange("(c t p) f -> c p t f", t=CT, p=P)
                        for c in range(NCH):
                            sp.wait_ge(kv_up, (c + 1) * CT // 2)
                            sp.dma_start(kv_[c], kv_stage[:, c % 2]).then_inc(kv_out[c % 2], 16)
                        for c in range(NCH):
                            sp.wait_ge(q_up, (c + 1) * CT // 2)
                            sp.dma_start(q_[c], q_parts[:, c % 2].rearrange("p t s d -> p t (s d)")
                                         ).then_inc(q_out[c % 2], 16)
                        sp.wait_ge(q_out[0], 16 * ((NCH + 1) // 2))
                        sp.wait_ge(q_out[1], 16 * (NCH // 2))
                    sp.wait_ge(rel_out, 16)

                    def loads(r, k, at):
                        g = U * r + k
                        if at >= NG:
                            return
                        if at >= 2:
                            sp.wait_ge(pick_done, g - 1)
                        sp.dma_start(rel[:, k % 2], rel_table[bass.ds(g, 1), :].broadcast_to([P, GE])
                                     ).then_inc(rel_in[k % 2], 16)
                        if at >= 2:
                            sp.wait_ge(e_done, g - 1)
                        sp.dma_start(ea[0:D, k % 2], eaT[bass.ds(g, 1)].rearrange("o d e -> (o d) e")
                                     ).then_inc(ea_in[k % 2], 16)
                        base = sp.value_load(base_int[0:1, bass.ds(g, 1)], min_val=0, max_val=NR - P)
                        if at >= 2:
                            sp.wait_ge(q_done, g - 1)
                        sp.dma_start(qwin[:, k % 2].rearrange("p s d -> p (s d)"), q_table[bass.ds(base, P), :]
                                     ).then_inc(qwin_in[k % 2], 16)

                    engine_turns(sp, loads)

                @block.gpsimd
                def _(pool):
                    if first:
                        nc.gpsimd.iota(node_id[:], pattern=[[0, 1]], base=0, channel_multiplier=1,
                                       allow_small_or_imprecise_dtypes=True).then_inc(ids_made, 1)
                        nc.gpsimd.iota(node_row[:], pattern=[[1, P]], base=0, channel_multiplier=0,
                                       allow_small_or_imprecise_dtypes=True).then_inc(ids_made, 1)
                        nc.gpsimd.memset(zeros[:], 0.0).then_inc(zero_set, 1)
                        pool.wait_ge(zero_set, 1)
                        pool.dma_start(acc_table.rearrange("(p t) f -> p (t f)", p=P), zeros[:]
                                       ).then_inc(acc_zeroed, 16)

                    def gathers(r, k, at):
                        if at >= NG:
                            return
                        g = U * r + k
                        if at >= 4:
                            pool.wait_ge(msg_done, g - 3)
                        pool.wait_ge(idx_in[k % 4], 16 * lap(r, k, 4))
                        pool.sem_inc(gathers_begun, 1)
                        for t in range(T if at < NG - 1 else LAST_TILES):
                            pool.indirect_dma_start(
                                kv[:, k % 4, t], None, kv_table,
                                bass.IndirectOffsetOnAxis(ap=idx[:, k % 4, t:t + 1], axis=0)
                            ).then_inc(kv_in[k % 4], 16)

                    if first:
                        pool.wait_ge(kv_out[0], 16 * ((NCH + 1) // 2))
                        pool.wait_ge(kv_out[1], 16 * (NCH // 2))
                    engine_turns(pool, gathers)

                @block.tensor
                def _(pe):
                    if first:
                        pe.wait_ge(w_in, 16)
                        pe.wait_ge(ones_set, 1)
                        for t in range(0, NR // P, 2):
                            n = t // 2
                            if t % CT < 2:
                                pe.wait_ge(xt_in[t // CT], 16)
                            if (t + 1) % CT == 0:
                                pe.wait_ge(xt_in[(t + 1) // CT], 16)
                            if n >= 4:
                                pe.wait_ge(kv_up, n - 3)
                            for j in range(2):
                                last = nc.tensor.matmul(kv_banks[n % 4][:, j * 2 * D:(j + 1) * 2 * D],
                                                        xt[0:DA, (t + j) * P:(t + j + 1) * P], wn[:, 0:2 * D],
                                                        start=True, stop=True)
                            last.then_inc(kv_mm, 1)
                        for t in range(0, NR // P, 2):
                            n = t // 2
                            if n >= 2:
                                pe.wait_ge(q_r, n - 1)
                                pe.wait_ge(q_hi, n - 1)
                            for j in range(2):
                                last = nc.tensor.matmul(psQ[:, n % 2, j * D:(j + 1) * D],
                                                        xt[0:DA, (t + j) * P:(t + j + 1) * P], wn[:, 2 * D:3 * D],
                                                        start=True, stop=True)
                            last.then_inc(q_mm, 1)
                        pe.wait_ge(we_in, 16)
                        pe.wait_ge(kv_up, NR // P // 2)
                        pe.wait_ge(q_r, NR // P // 2)
                        pe.wait_ge(q_hi, NR // P // 2)

                    def products(r, k, at):
                        g = U * r + k
                        if at < NG:
                            pe.wait_ge(qwin_in[k % 2], 16 * lap(r, k, 2))
                            pe.wait_ge(pick_done, g + 1)
                            if at >= 1:
                                pe.wait_ge(qk_done, g)
                            for t in range(T):
                                for s in range(3):
                                    last = nc.tensor.matmul(
                                        psQ[:, t // 4, (t % 4) * D:(t % 4 + 1) * D],
                                        pick[:, k % 2, t * P:(t + 1) * P], qwin[:, k % 2, s],
                                        start=(s == 0), stop=(s == 2))
                            last.then_inc(q_done, 1)
                            pe.wait_ge(ea_in[k % 2], 16 * lap(r, k, 2))
                            if at >= 1:
                                pe.wait_ge(qke_done, g)
                            for t in range(T):
                                last = nc.tensor.matmul(
                                    psE[:, t // 4, (t % 4) * D:(t % 4 + 1) * D],
                                    ea[:, k % 2, t * P:(t + 1) * P], we[:], start=True, stop=True)
                            last.then_inc(e_done, 1)
                        if 1 <= at <= NG:
                            pe.wait_ge(msg_done, g)
                            pe.wait_ge(place_done, g)
                            pe.wait_ge(wt_done, g)
                            if at >= 3:
                                pe.wait_ge(merge_done, g - 2)
                            s = (k - 1) % 2
                            for t in range(T):
                                last = nc.tensor.matmul(psA[:, s, 0:ML], place[:, s, t], msg[:, s, t],
                                                        start=(t == 0), stop=(t == T - 1))
                            last.then_inc(sum_done, 1)

                    engine_turns(pe, products)

                @block.scalar
                def _(act):
                    for g in range(4):
                        act.dma_start(idx[:, g], src[g]).then_inc(idx_in[g], 16)
                    if first:
                        for n in range(NR // P // 2):
                            t = 2 * n
                            if t % CT < 2 and t // CT >= 2:
                                c = t // CT
                                act.wait_ge(kv_out[c % 2], 16 * (c // 2))
                            act.wait_ge(kv_mm, n + 1)
                            nc.scalar.activation(
                                kv_stage[:, (t // CT) % 2, t % CT:t % CT + 2],
                                kv_banks[n % 4][:, 0:4 * D].rearrange("p (j f) -> p j f", j=2), ACT.Copy
                            ).then_inc(kv_up, 1)
                        for n in range(NR // P // 2):
                            t = 2 * n
                            c, u = t // CT, t % CT
                            if u < 2 and c >= 2:
                                act.wait_ge(q_out[c % 2], 16 * (c // 2))
                            act.wait_ge(q_mm, n + 1)
                            nc.scalar.activation(
                                q_parts[:, c % 2, u:u + 2, 0],
                                psQ[:, n % 2, 0:2 * D].rearrange("p (j f) -> p j f", j=2), ACT.Copy,
                                scale=float(HD) ** -0.5).then_inc(q_hi, 1)
                            act.wait_ge(q_r, n + 1)
                            nc.scalar.activation(q_parts[:, c % 2, u:u + 2, 1], q_rest[:, n % 2],
                                                 ACT.Copy).then_inc(q_mid, 1)
                        act.wait_ge(acc_zeroed, 16)
                    act.wait_ge(tables_up, 1)

                    def base_of(g):
                        return act.value_load(base_int[0:1, bass.ds(g, 1)], min_val=0, max_val=NR - P)

                    def weights(r, k, at):
                        g = U * r + k
                        if at < NG:
                            act.wait_ge(clip_done, g + 1)
                            if at >= 1:
                                act.wait_ge(msg_done, g)
                            nc.scalar.activation(ps_wt, clipped[:, k % 2], ACT.Exp).then_inc(exp_done, 1)
                            if at >= 2:
                                act.wait_ge(sum_done, g - 1)
                            nc.scalar.activation(msg[:, k % 2, :, D:ML],
                                                 clipped[:, k % 2].rearrange("p (t h) -> p t h", t=T),
                                                 ACT.Exp).then_inc(wt_done, 1)
                            if at + 4 < NG:
                                act.dma_start(idx[:, k % 4], src[bass.ds(g + 4, 1)].rearrange("o p t -> (o p) t")
                                              ).then_inc(idx_in[k % 4], 16)
                        if 2 <= at:
                            base = base_of(g - 2)
                            act.wait_ge(merge_done, g - 1)
                            act.dma_start(acc_table[bass.ds(base, P), :], accw[:, k % 2]
                                          ).then_inc(accw_out[k % 2], 16)
                        if 1 <= at <= NG:
                            base = base_of(g - 1)
                            if at >= 2:
                                act.wait_ge(accw_out[k % 2], 16 * lap(r, k - 2, 2))
                            act.dma_start(accw[:, (k - 1) % 2], acc_table[bass.ds(base, P), :]
                                          ).then_inc(accw_in[(k - 1) % 2], 16)

                    engine_turns(act, weights)
                    act.wait_ge(accw_out[(NG - 1) % 2], 16 * ((NG - 1) // 2 + 1))

                @block.vector
                def _(dve):
                    chained = [0]

                    def link(ins):
                        chained[0] += 1
                        ins.then_inc(tables_chain, 1)
                        dve.wait_ge(tables_chain, chained[0])

                    if first:
                        nc.vector.memset(xt[D:DA, :], 1.0)
                        nc.vector.memset(ea[D:DA, :, :], 1.0).then_inc(ones_set, 1)
                        dve.wait_ge(ids_made, 2)
                        nc.vector.tensor_copy(ps_ids, node_row[:]).then_inc(ids_up, 1)
                        dve.wait_ge(dst_in, 32)
                        nc.vector.tensor_reduce(ranges[:, 0:1], dstg[:], AX.X, ALU.min)
                        link(nc.vector.scalar_tensor_tensor(out=dst_masked[:], in0=dstg[:], scalar=float(N),
                                                            in1=dstg[:], op0=ALU.is_lt, op1=ALU.mult))
                        link(nc.vector.tensor_reduce(ranges[:, 2:3], dst_masked[:], AX.X, ALU.max))
                        nc.vector.tensor_tensor(ranges[:, 1:2], ranges[:, 2:3], ranges[:, 0:1],
                                                ALU.subtract).then_inc(range_up, 1)
                        dve.wait_ge(range_in, 16)
                        link(nc.vector.reduce_max(fits[:, 0:1], ranges_all[:, :, 1], AX.X))
                        link(nc.vector.tensor_scalar(fits[:, 1:2], fits[:, 0:1], float(P), None, ALU.is_lt))
                        nc.vector.tensor_scalar(base_all[:], ranges_all[:, :, 0], fits[:, 1:2], None, ALU.mult)
                        nc.vector.tensor_scalar(flag_int[:], fits[:, 1:2], -1.0, 1.0, ALU.mult, ALU.add)
                        nc.vector.memset(window[:], 0.0)
                        link(nc.vector.tensor_scalar(ranges[:, 3:4], ranges[:, 0:1], fits[0:NG, 1:2], None,
                                                     ALU.mult))
                    else:
                        link(nc.vector.tensor_scalar(window[:], window[:], float(P), None, ALU.add))
                        nc.vector.tensor_scalar(base_all[:], base_all[:], 0.0, window[:], ALU.mult, ALU.add)
                        link(nc.vector.tensor_copy(ranges[:, 3:4], window[0:NG, :]))
                    nc.vector.tensor_copy(base_int[:], base_all[:])
                    nc.vector.tensor_scalar(rel_group[:], dstg[:], ranges[:, 3:4], None, ALU.subtract)
                    link(nc.vector.tensor_tensor(rel_tile[:].rearrange("p (g t) -> p g t", t=T),
                                                 dstp[:].rearrange("p (g t) -> p g t", t=T),
                                                 base_all[:].unsqueeze(2).broadcast_to([P, NG, T]),
                                                 ALU.subtract))
                    dve.sem_inc(tables_up, 1)
                    if first:
                        for n in range(NR // P // 2):
                            t = 2 * n
                            c, u = t // CT, t % CT
                            dve.wait_ge(q_hi, n + 1)
                            nc.vector.scalar_tensor_tensor(
                                out=q_rest[:, n % 2], in0=psQ[:, n % 2, 0:2 * D].rearrange("p (j f) -> p j f", j=2),
                                scalar=float(HD) ** -0.5, in1=q_parts[:, c % 2, u:u + 2, 0],
                                op0=ALU.mult, op1=ALU.subtract).then_inc(q_r, 1)
                            dve.wait_ge(q_mid, n + 1)
                            nc.vector.tensor_tensor(q_parts[:, c % 2, u:u + 2, 2], q_rest[:, n % 2],
                                                    q_parts[:, c % 2, u:u + 2, 1],
                                                    ALU.subtract).then_inc(q_up, 1)

                    def make_pick(r, k, at):
                        g = U * r + k
                        dve.wait_ge(rel_in[k % 2], 16 * lap(r, k, 2))
                        if at >= 2:
                            dve.wait_ge(q_done, g - 1)
                        nc.vector.tensor_scalar(pick[:, k % 2], rel[:, k % 2], node_id[:], None,
                                                ALU.is_equal).then_inc(pick_done, 1)

                    def arithmetic(r, k, at):
                        g = U * r + k
                        s, was = k % 2, (k - 1) % 2
                        if at + 1 < NG:
                            make_pick(r, k + 1, at + 1)
                        if 1 <= at <= NG:
                            dve.wait_ge(exp_done, g)
                            if at >= 3:
                                dve.wait_ge(sum_done, g - 2)
                            nc.vector.tensor_tensor(
                                msg[:, was, :, 0:D].rearrange("p t (h d) -> p t h d", h=H),
                                kv[:, (k - 1) % 4, :, D:2 * D].rearrange("p t (h d) -> p t h d", h=H),
                                ps_wt.rearrange("p (t h) -> p t h", t=T).unsqueeze(3)
                                .broadcast_to([P, T, H, HD]), ALU.mult).then_inc(msg_done, 1)
                        if at < NG:
                            gathered = 16 * T * lap(r, k, 4)
                            if at == NG - 1:
                                gathered -= 16 * (T - LAST_TILES)
                            dve.wait_ge(kv_in[k % 4], gathered)
                            dve.wait_ge(q_done, g + 1)
                            if at >= 1:
                                dve.wait_ge(qke_done, g)
                            nc.vector.tensor_tensor(
                                qk[:].rearrange("p (b t) d -> p b t d", b=2),
                                psQ[:, :, 0:4 * D].rearrange("p b (t d) -> p b t d", t=4),
                                kv[:, k % 4, :, 0:D].rearrange("p (b t) d -> p b t d", b=2),
                                ALU.mult).then_inc(qk_done, 1)
                            if at >= 2:
                                dve.wait_ge(sum_done, g - 1)
                            nc.vector.tensor_tensor(
                                place[:, s], ps_ids.unsqueeze(1).broadcast_to([P, T, P]),
                                rel_tile[:, bass.ds(g * T, T)].unsqueeze(2).broadcast_to([P, T, P]),
                                ALU.is_equal).then_inc(place_done, 1)
                            dve.wait_ge(e_done, g + 1)
                            dve.wait_ge(qk_done, g + 1)
                            if at >= 1:
                                dve.wait_ge(logit_done, g)
                            nc.vector.tensor_tensor(
                                qke[:].rearrange("p (b t) d -> p b t d", b=2),
                                psE[:, :, 0:4 * D].rearrange("p b (t d) -> p b t d", t=4),
                                qk[:].rearrange("p (b t) d -> p b t d", b=2), ALU.mult).then_inc(qke_done, 1)
                        if 2 <= at:
                            dve.wait_ge(sum_done, g - 1)
                            dve.wait_ge(accw_in[s], 16 * lap(r, k - 2, 2))
                            nc.vector.tensor_tensor(accw[:, s], psA[:, s, 0:ML], accw[:, s],
                                                    ALU.add).then_inc(merge_done, 1)
                        if at < NG:
                            dve.wait_ge(qke_done, g + 1)
                            if at >= 1:
                                dve.wait_ge(clip_done, g)
                            nc.vector.tensor_reduce(logit[:], qke[:].rearrange("p t (h d) -> p (t h) d", h=H),
                                                    AX.X, ALU.add).then_inc(logit_done, 1)
                            dve.wait_ge(logit_done, g + 1)
                            if at >= 2:
                                dve.wait_ge(wt_done, g - 1)
                            nc.vector.tensor_scalar(clipped[:, s], logit[:], -5.0, 5.0, ALU.max,
                                                    ALU.min).then_inc(clip_done, 1)

                    make_pick(0, 0, 0)
                    engine_turns(dve, arithmetic)

        def clear_all():
            nc.all_engine_barrier(sems_to_clear=range(sems[0].num, sems[-1].num + 1))

        edge_pass(True)
        clear_all()
        spans_more = nc.values_load(flag_int[0:1, 0:1], min_val=0, max_val=1)
        with nc.If(spans_more > 0):
            with nc.Fori(1, NW):
                edge_pass(False)
                clear_all()

        hsum = zeros[:, 0:OT * ML].rearrange("p (t f) -> p t f", t=OT)
        xr = sb("xr", [P, OT, D], f32)
        y = xt[:, 0:OT * D].rearrange("p (t f) -> p t f", t=OT)
        y2 = kv[:].rearrange("p s t f -> p (s t f)")[:, 0:OT * D].rearrange("p (t f) -> p t f", t=OT)
        rz = sb("rz", [P, OT, H], f32)
        st = sb("st", [P, 6, OT], f32)
        with nc.Block() as block:
            ein, eout, elink, esq = epi[0], epi[1], epi[2], epi[3]
            esd, eact = epi[4], epi[5]

            @block.sync
            def _(sp):
                sp.dma_start(hsum[:], acc_table[0:NW * P, :].rearrange("(p t) f -> p t f", p=P)).then_inc(ein, 16)
                sp.dma_start(xr[:], xrows.rearrange("(p t) f -> p t f", p=P)).then_inc(ein, 16)
                sp.wait_ge(esd, 1)
                sp.dma_start(out.rearrange("(p t) f -> p t f", p=P), y[:]).then_inc(eout, 16)
                sp.wait_ge(eout, 16)

            @block.scalar
            def _(act):
                act.wait_ge(esq, 1)
                nc.scalar.activation(y2[:], y[:], ACT.Square).then_inc(eact, 1)
                act.wait_ge(esq, 2)
                nc.scalar.activation(st[:, 3], st[:, 2], ACT.Sqrt).then_inc(eact, 1)

            @block.vector
            def _(dve):
                n = [0]

                def link(ins):
                    n[0] += 1
                    ins.then_inc(elink, 1)
                    dve.wait_ge(elink, n[0])
                dve.wait_ge(ein, 32)
                link(nc.vector.tensor_scalar(rz[:], hsum[:, :, D:ML], EPS_Z, None, ALU.add))
                link(nc.vector.reciprocal(rz[:], rz[:]))
                link(nc.vector.tensor_tensor(y[:].rearrange("p t (h d) -> p t h d", h=H),
                                             hsum[:, :, 0:D].rearrange("p t (h d) -> p t h d", h=H),
                                             rz[:].unsqueeze(3).broadcast_to([P, OT, H, HD]), ALU.mult))
                link(nc.vector.tensor_tensor(y[:], y[:], xr[:], ALU.add))
                link(nc.vector.reduce_sum(st[:, 0], y[:], AX.X))
                link(nc.vector.tensor_scalar(st[:, 1], st[:, 0], 1.0 / D, None, ALU.mult))
                nc.vector.tensor_tensor(y[:], y[:], st[:, 1].unsqueeze(2).broadcast_to([P, OT, D]),
                                        ALU.subtract).then_inc(esq, 1)
                dve.wait_ge(eact, 1)
                link(nc.vector.reduce_sum(st[:, 0], y2[:], AX.X))
                nc.vector.tensor_scalar(st[:, 2], st[:, 0], 1.0 / D, EPS_LN, ALU.mult, ALU.add).then_inc(esq, 1)
                dve.wait_ge(eact, 2)
                link(nc.vector.reciprocal(st[:, 4], st[:, 3]))
                nc.vector.tensor_tensor(y[:], y[:], st[:, 4].unsqueeze(2).broadcast_to([P, OT, D]),
                                        ALU.mult).then_inc(esd, 1)


def kernel(x, src, dst, edge_attr_96, L0_gnn_Wq, L0_gnn_bq, L0_gnn_Wk, L0_gnn_bk, L0_gnn_We, L0_gnn_be,
           L0_gnn_Wv, L0_gnn_bv):
    import numpy as np
    import concourse.bacc as bacc
    from concourse.bass_utils import run_bass_kernel_spmd

    x, src, dst, ea = (np.asarray(a) for a in (x, src, dst, edge_attr_96))
    wq, bq, wk, bk, we, be, wv, bv = (np.asarray(a) for a in (
        L0_gnn_Wq, L0_gnn_bq, L0_gnn_Wk, L0_gnn_bk, L0_gnn_We, L0_gnn_be, L0_gnn_Wv, L0_gnn_bv))
    xT = np.zeros((D, NR), x.dtype)
    xT[:, :N] = x.T
    xrows = np.zeros((NW * P, D), x.dtype)
    xrows[:N] = x
    src_pad = np.zeros(NG * GE, src.dtype)
    src_pad[:E] = src
    dst_pad = np.full(NG * GE, N, dst.dtype)
    dst_pad[:E] = dst
    eaT = np.zeros((NG * GE, D), ea.dtype)
    eaT[:E] = ea
    arrays = {
        "xT": xT,
        "xrows": xrows,
        "src": np.ascontiguousarray(src_pad.reshape(NG, T, P).transpose(0, 2, 1)),
        "dst_group": dst_pad.reshape(NG, GE),
        "dst_tile": np.ascontiguousarray(dst_pad.reshape(NG * T, P).T),
        "eaT": np.ascontiguousarray(eaT.reshape(NG, GE, D).transpose(0, 2, 1)),
        "w_node": np.concatenate([np.concatenate([wk, wv, wq], 1), np.concatenate([bk, bv, bq])[None]], 0),
        "w_edge": np.concatenate([we, be[None]], 0),
    }
    nc = bacc.Bacc("TRN2", target_bir_lowering=False, num_devices=1)
    args = [nc.dram_tensor(n, a.shape, mybir.dt.from_np(a.dtype), kind="ExternalInput").ap()
            for n, a in arrays.items()]
    out = nc.dram_tensor("out", (NW * P, D), mybir.dt.float32, kind="ExternalOutput").ap()
    gnn_program(nc, *args, out)
    r = run_bass_kernel_spmd(nc, [arrays], core_ids=[0])
    return r.results[0]["out"][:N]
```

```python
import concourse.bass as bass
from concourse import mybir
from contextlib import ExitStack

P = 128
N = 6250
E = 100000
D = 96
H = 8
HD = D // H
DA = D + 1
T = 8
GE = T * P
NG = -(-E // GE)
LAST_TILES = -(-E // P) - (NG - 1) * T
NW = -(-N // P)
NR = (NW + 1) * P
ML = D + H
EPS_Z = 1e-6
EPS_LN = 1e-5
U = 4
TURNS = (NG - 4) // U
NCH = 5
CT = NR // P // NCH
OT = NW
QB = 5
MEAN_STEPS, OUT_STEPS = 5, 6


def lap(r, k, ring):
    return (U // ring) * r + k // ring + 1


def gnn_program(nc, xT, ones, xrows, src, dst_group, dst_tile, eaT, w_node, w_edge, out):
    f32, bf16, i32 = mybir.dt.float32, mybir.dt.bfloat16, mybir.dt.int32
    ALU, ACT, AX = mybir.AluOpType, mybir.ActivationFunctionType, mybir.AxisListType

    kv_table = nc.dram_tensor("kv_table", (NR, 2 * D), f32, kind="Internal").ap()
    q_table = nc.dram_tensor("q_table", (NR, 3 * D), bf16, kind="Internal").ap()
    rel_table = nc.dram_tensor("rel_table", (NG, GE), bf16, kind="Internal").ap()
    range_table = nc.dram_tensor("range_table", (NG, 2), f32, kind="Internal").ap()
    acc_table = nc.dram_tensor("acc_table", (NR, ML), f32, kind="Internal").ap()

    ctx = ExitStack()
    with ctx:
        def sb(name, shape, dt):
            return ctx.enter_context(nc.sbuf_tensor(name, shape, dt))

        def ps(name, shape, dt):
            return ctx.enter_context(nc.psum_tensor(name, shape, dt))

        sems = []

        def sem(name):
            sems.append(ctx.enter_context(nc.semaphore(name)))
            return sems[-1]

        wn = sb("wn", [DA, 3 * D], f32)
        we = sb("we", [DA, D], f32)
        xt = sb("xt", [P, NR], f32)
        kv_stage = sb("kv_stage", [P, NR // P, 2 * D], f32)
        q_parts = sb("q_parts", [P, NR // P, 3, D], bf16)
        q_rest = sb("q_rest", [P, 2, QB, D], f32)
        zeros = sb("zeros", [P, NR // P * ML], f32)
        dstg = sb("dstg", [NG, GE], i32)
        dstp = sb("dstp", [P, NG * T], i32)
        dst_masked = sb("dst_masked", [NG, GE], f32)
        ranges = sb("ranges", [NG, 4], f32)
        ranges_all = sb("ranges_all", [P, NG, 2], f32)
        steps = sb("steps", [P, NG + 1], f32)
        checks = sb("checks", [P, 8], f32)
        base_all = sb("base_all", [P, NG], f32)
        base_int = sb("base_int", [P, NG], i32)
        left_int = sb("left_int", [P, 1], i32)
        window = sb("window", [P, 1], f32)
        rel_group = sb("rel_group", [NG, GE], bf16)
        rel_tile = sb("rel_tile", [P, NG * T], bf16)
        node_id = sb("node_id", [P, 1], f32)
        node_row = sb("node_row", [P, P], f32)
        idx = sb("idx", [P, 4, T], i32)
        kv = kv_stage[:, 0:4 * T, :].rearrange("p (s t) f -> p s t f", s=4)
        ea = sb("ea", [DA, 2, GE], f32)
        rel = sb("rel", [P, 4, GE], bf16)
        qwin = sb("qwin", [P, 2, 3, D], bf16)
        xwin = sb("xwin", [P, 4, D], f32)
        pick = sb("pick", [P, 2, GE], bf16)
        place = sb("place", [P, 2, T, P], f32)
        qk = sb("qk", [P, T, D], f32)
        qke = sb("qke", [P, T, D], f32)
        logit = sb("logit", [P, T * H], f32)
        clipped = sb("clipped", [P, 2, T * H], f32)
        msg = sb("msg", [P, 2, T, ML], f32)
        accw = sb("accw", [P, 2, ML], f32)
        rz = sb("rz", [P, 2, H], f32)
        hw = sb("hw", [P, D], f32)
        yw = sb("yw", [P, 2, D], f32)
        outw = sb("outw", [P, 2, D], f32)
        bn = sb("bn", [P, 6], f32)
        stat = sb("stat", [P, 8], f32)
        psE = ps("psE", [P, 2, 512], f32)
        psQ = ps("psQ", [P, 2, 512], f32)
        psA = ps("psA", [P, 2, 512], f32)
        psI = ps("psI", [P, 512], f32)
        psW = ps("psW", [P, 512], f32)
        ps_ids = psI[:, 0:P]
        ps_wt = psW[:, 0:T * H]
        kv_banks = [psE[:, 0], psE[:, 1], psA[:, 0], psA[:, 1]]
        q_banks = [psQ[:, 0], psQ[:, 1], psW[:, :], psE[:, 0]]

        w_in, we_in, dst_in, ones_in = sem("w_in"), sem("we_in"), sem("dst_in"), sem("ones_in")
        xt_in = [sem(f"xt_in{c}") for c in range(NCH)]
        ids_made, ids_up, zero_set = sem("ids_made"), sem("ids_up"), sem("zero_set")
        kv_mm, kv_up, kv_out = sem("kv_mm"), sem("kv_up"), sem("kv_out")
        q_mm, q_hi, q_r, q_mid, q_up = sem("q_mm"), sem("q_hi"), sem("q_r"), sem("q_mid"), sem("q_up")
        q_out = sem("q_out")
        acc_zeroed = sem("acc_zeroed")
        range_up, range_out, range_in = sem("range_up"), sem("range_out"), sem("range_in")
        tables_chain, tables_up, rel_out = sem("tables_chain"), sem("tables_up"), sem("rel_out")

        idx_in = [sem(f"idx_in{i}") for i in range(4)]
        kv_in = [sem(f"kv_in{i}") for i in range(4)]
        ea_in = [sem(f"ea_in{i}") for i in range(2)]
        rel_in = [sem(f"rel_in{i}") for i in range(4)]
        qwin_in = [sem(f"qwin_in{i}") for i in range(2)]
        xwin_in = [sem(f"xwin_in{i}") for i in range(4)]
        accw_in = [sem(f"accw_in{i}") for i in range(2)]
        accw_out = [sem(f"accw_out{i}") for i in range(2)]
        out_out = [sem(f"out_out{i}") for i in range(2)]
        e_done, q_done, sum_done = sem("e_done"), sem("q_done"), sem("sum_done")
        pick_done, place_done, qk_done, qke_done = sem("pick_done"), sem("place_done"), sem("qk_done"), sem("qke_done")
        logit_done, clip_done, msg_done, merge_done = sem("logit_done"), sem("clip_done"), sem("msg_done"), sem("merge_done")
        exp_done, wt_done = sem("exp_done"), sem("wt_done")
        mean_steps, out_steps, log_done, root_done, fin_done = sem("mean_steps"), sem("out_steps"), sem("log_done"), sem("root_done"), sem("fin_done")
        gathers_begun, outs_begun = sem("gathers_begun"), sem("outs_begun")

        def engine_turns(eng, body):
            for k in range(U):
                body(0, k, k)
            with eng.Fori(1, TURNS) as r:
                for k in range(U):
                    body(r, k, U + k)
            for at in range(TURNS * U, NG + 2):
                body(TURNS, at - TURNS * U, at)

        def edge_pass(first):
            def load_rel(eng, r, k):
                eng.dma_start(rel[:, k % 4], rel_table[bass.ds(U * r + k, 1), :].broadcast_to([P, GE])
                              ).then_inc(rel_in[k % 4], 16)

            def load_ea(eng, r, k):
                eng.dma_start(ea[0:D, k % 2], eaT[bass.ds(U * r + k, 1)].rearrange("o d e -> (o d) e")
                              ).then_inc(ea_in[k % 2], 16)

            def load_windows(eng, r, k):
                base = eng.value_load(base_int[0:1, bass.ds(U * r + k, 1)], min_val=0, max_val=NR - P)
                eng.dma_start(qwin[:, k % 2].rearrange("p s d -> p (s d)"), q_table[bass.ds(base, P), :]
                              ).then_inc(qwin_in[k % 2], 16)
                if first:
                    eng.dma_start(xwin[:, k % 4], xrows[bass.ds(base, P), :]).then_inc(xwin_in[k % 4], 16)

            with nc.Block() as block:

                @block.sync
                def _(sp):
                    if first:
                        sp.dma_start(wn[:], w_node).then_inc(w_in, 16)
                        for c in range(NCH):
                            cols = slice(c * CT * P, (c + 1) * CT * P)
                            sp.dma_start(xt[0:D, cols], xT[:, cols]).then_inc(xt_in[c], 16)
                            if c == 0:
                                sp.dma_start(xt[D:DA, :], ones).then_inc(ones_in, 16)
                                sp.dma_start(dstg[:], dst_group).then_inc(dst_in, 16)
                                sp.dma_start(dstp[:], dst_tile).then_inc(dst_in, 16)
                        sp.dma_start(we[:], w_edge).then_inc(we_in, 16)
                        for s in range(2):
                            sp.dma_start(ea[D:DA, s], ones[:, 0:GE]).then_inc(we_in, 16)
                        kv_ = kv_table.rearrange("(c t p) f -> c p t f", t=CT, p=P)
                        q_ = q_table.rearrange("(c t p) f -> c p t f", t=CT, p=P)
                        for c in range(NCH):
                            sp.wait_ge(kv_up, (c + 1) * CT // 2)
                            sp.dma_start(kv_[c], kv_stage[:, c * CT:(c + 1) * CT]).then_inc(kv_out, 16)
                    sp.wait_ge(rel_out, 16)
                    for g in range(3):
                        load_rel(sp, 0, g)
                    for g in range(2):
                        load_ea(sp, 0, g)
                    if first:
                        for c in range(NCH):
                            sp.wait_ge(q_up, (c + 1) * CT // QB)
                            sp.dma_start(q_[c], q_parts[:, c * CT:(c + 1) * CT].rearrange("p t s d -> p t (s d)")
                                         ).then_inc(q_out, 16)
                        sp.wait_ge(q_out, 16 * NCH)
                    for g in range(2):
                        load_windows(sp, 0, g)
                    if first:
                        sp.wait_ge(zero_set, 1)
                        sp.dma_start(acc_table.rearrange("(p t) f -> p (t f)", p=P), zeros[:]
                                     ).then_inc(acc_zeroed, 16)
                        sp.wait_ge(acc_zeroed, 16)

                    def base_of(g):
                        return sp.value_load(base_int[0:1, bass.ds(g, 1)], min_val=0, max_val=NR - P)

                    def sums(r, k, at):
                        g = U * r + k
                        s = k % 2
                        if at < NG:
                            base = base_of(g)
                            sp.wait_ge(merge_done, g + 1)
                            sp.dma_start(acc_table[bass.ds(base, P), :], accw[:, s]).then_inc(accw_out[s], 16)
                        if at + 1 < NG:
                            base = base_of(g + 1)
                            sp.wait_ge(accw_out[s], 16 * lap(r, k, 2))
                            sp.dma_start(accw[:, 1 - s], acc_table[bass.ds(base, P), :]
                                         ).then_inc(accw_in[1 - s], 16)
                        if first and at >= 2:
                            base = base_of(g - 2)
                            if at >= 3:
                                sp.wait_ge(out_out[1 - s], 16 * lap(r, k - 3, 2))
                                sp.sem_inc(outs_begun, 1)
                            sp.wait_ge(fin_done, g - 1)
                            sp.dma_start(out[bass.ds(base, P), :], outw[:, s]).then_inc(out_out[s], 16)

                    sp.dma_start(accw[:, 0], acc_table[bass.ds(base_of(0), P), :]).then_inc(accw_in[0], 16)
                    engine_turns(sp, sums)
                    for s in range(2):
                        sp.wait_ge(accw_out[s], 16 * ((NG - s + 1) // 2))
                        if first:
                            sp.wait_ge(out_out[s], 16 * ((NG - s + 1) // 2))

                @block.gpsimd
                def _(pool):
                    if first:
                        nc.gpsimd.iota(node_id[:], pattern=[[0, 1]], base=0, channel_multiplier=1,
                                       allow_small_or_imprecise_dtypes=True).then_inc(ids_made, 1)
                        nc.gpsimd.iota(node_row[:], pattern=[[1, P]], base=0, channel_multiplier=0,
                                       allow_small_or_imprecise_dtypes=True).then_inc(ids_made, 1)
                        nc.gpsimd.memset(zeros[:], 0.0).then_inc(zero_set, 1)
                        pool.wait_ge(range_up, 1)
                        pool.dma_start(range_table, ranges[:, 0:2]).then_inc(range_out, 16)
                        pool.wait_ge(range_out, 16)
                        pool.dma_start(ranges_all[:].rearrange("p g c -> p (g c)"),
                                       range_table.rearrange("g c -> (g c)").unsqueeze(0).broadcast_to([P, NG * 2])
                                       ).then_inc(range_in, 16)
                    pool.wait_ge(tables_up, 1)
                    pool.dma_start(rel_table, rel_group[:]).then_inc(rel_out, 16)
                    if first:
                        pool.wait_ge(kv_out, 16 * NCH)

                    def gathers(r, k, at):
                        if at >= NG:
                            return
                        g = U * r + k
                        if at >= 4:
                            pool.wait_ge(msg_done, g - 3)
                        pool.wait_ge(idx_in[k % 4], 16 * lap(r, k, 4))
                        pool.sem_inc(gathers_begun, 1)
                        for t in range(T if at < NG - 1 else LAST_TILES):
                            pool.indirect_dma_start(
                                kv[:, k % 4, t], None, kv_table,
                                bass.IndirectOffsetOnAxis(ap=idx[:, k % 4, t:t + 1], axis=0)
                            ).then_inc(kv_in[k % 4], 16)

                    engine_turns(pool, gathers)
                    for s in range(4):
                        left = (T - LAST_TILES) if s == (NG - 1) % 4 else 0
                        pool.wait_ge(kv_in[s], 16 * (T * len(range(s, NG, 4)) - left))
                    if first:
                        pool.wait_ge(range_in, 16)
                    pool.wait_ge(rel_out, 16)
                    nc.gpsimd.dma_reset()

                @block.tensor
                def _(pe):
                    if first:
                        pe.wait_ge(w_in, 16)
                        pe.wait_ge(ones_in, 16)
                        for t in range(0, NR // P, 2):
                            n = t // 2
                            if t % CT < 2:
                                pe.wait_ge(xt_in[t // CT], 16)
                            if n >= 4:
                                pe.wait_ge(kv_up, n - 3)
                            for j in range(2):
                                last = nc.tensor.matmul(kv_banks[n % 4][:, j * 2 * D:(j + 1) * 2 * D],
                                                        xt[0:DA, (t + j) * P:(t + j + 1) * P], wn[:, 0:2 * D],
                                                        start=True, stop=True)
                            last.then_inc(kv_mm, 1)
                        pe.wait_ge(kv_up, NR // P // 2)
                        for n in range(NR // P // QB):
                            if n >= 4:
                                pe.wait_ge(q_r, n - 3)
                            for j in range(QB):
                                t = n * QB + j
                                last = nc.tensor.matmul(q_banks[n % 4][:, j * D:(j + 1) * D],
                                                        xt[0:DA, t * P:(t + 1) * P], wn[:, 2 * D:3 * D],
                                                        start=True, stop=True)
                            last.then_inc(q_mm, 1)
                        pe.wait_ge(we_in, 48)
                        pe.wait_ge(q_r, NR // P // QB)

                    def to_edges(r, k, at):
                        g = U * r + k
                        pe.wait_ge(qwin_in[k % 2], 16 * lap(r, k, 2))
                        pe.wait_ge(pick_done, g + 1)
                        if at >= 1:
                            pe.wait_ge(qk_done, g)
                        for t in range(T):
                            for s in range(3):
                                last = nc.tensor.matmul(
                                    psQ[:, t // 4, (t % 4) * D:(t % 4 + 1) * D],
                                    pick[:, k % 2, t * P:(t + 1) * P], qwin[:, k % 2, s],
                                    start=(s == 0), stop=(s == 2))
                        last.then_inc(q_done, 1)
                        pe.wait_ge(ea_in[k % 2], 16 * lap(r, k, 2))
                        if at >= 1:
                            pe.wait_ge(qke_done, g)
                        for t in range(T):
                            last = nc.tensor.matmul(
                                psE[:, t // 4, (t % 4) * D:(t % 4 + 1) * D],
                                ea[:, k % 2, t * P:(t + 1) * P], we[:], start=True, stop=True)
                        last.then_inc(e_done, 1)

                    def products(r, k, at):
                        g = U * r + k
                        if at + 1 < NG:
                            to_edges(r, k + 1, at + 1)
                        if at < NG:
                            s = k % 2
                            pe.wait_ge(place_done, g + 1)
                            pe.wait_ge(wt_done, g + 1)
                            if at >= 2:
                                pe.wait_ge(merge_done, g - 1)
                            pe.wait_ge(msg_done, g + 1)
                            for t in range(T):
                                last = nc.tensor.matmul(psA[:, s, 0:ML], place[:, s, t], msg[:, s, t],
                                                        start=(t == 0), stop=(t == T - 1))
                            last.then_inc(sum_done, 1)

                    to_edges(0, 0, 0)
                    engine_turns(pe, products)

                @block.scalar
                def _(act):
                    for g in range(4):
                        act.dma_start(idx[:, g], src[g]).then_inc(idx_in[g], 16)
                    if first:
                        nc.scalar.preload_act_table_set("natural_log_exp_and_others")
                        for n in range(NR // P // 2):
                            act.wait_ge(kv_mm, n + 1)
                            nc.scalar.activation(
                                kv_stage[:, 2 * n:2 * n + 2],
                                kv_banks[n % 4][:, 0:4 * D].rearrange("p (j f) -> p j f", j=2), ACT.Copy
                            ).then_inc(kv_up, 1)

                    if first:
                        def leading(n):
                            act.wait_ge(q_mm, n + 1)
                            nc.scalar.activation(
                                q_parts[:, n * QB:(n + 1) * QB, 0],
                                q_banks[n % 4][:, 0:QB * D].rearrange("p (j f) -> p j f", j=QB), ACT.Copy,
                                scale=float(HD) ** -0.5).then_inc(q_hi, 1)

                        leading(0)
                        for n in range(NR // P // QB):
                            if n + 1 < NR // P // QB:
                                leading(n + 1)
                            act.wait_ge(q_r, n + 1)
                            nc.scalar.activation(q_parts[:, n * QB:(n + 1) * QB, 1], q_rest[:, n % 2],
                                                 ACT.Copy).then_inc(q_mid, 1)

                    def weights(r, k, at):
                        g = U * r + k
                        if first and at >= 2:
                            act.wait_ge(out_steps, OUT_STEPS * (g - 2) + 3)
                            nc.scalar.activation(stat[:, 3:4], stat[:, 2:3], ACT.Ln).then_inc(log_done, 1)
                            act.wait_ge(log_done, g - 1)
                            nc.scalar.activation(stat[:, 4:5], stat[:, 3:4], ACT.Exp, scale=-0.5
                                                 ).then_inc(root_done, 1)
                        if at < NG:
                            act.wait_ge(clip_done, g + 1)
                            if at >= 1:
                                act.wait_ge(msg_done, g)
                            nc.scalar.activation(ps_wt, clipped[:, k % 2], ACT.Exp).then_inc(exp_done, 1)
                            if at >= 2:
                                act.wait_ge(sum_done, g - 1)
                            nc.scalar.activation(msg[:, k % 2, :, D:ML],
                                                 clipped[:, k % 2].rearrange("p (t h) -> p t h", t=T),
                                                 ACT.Exp).then_inc(wt_done, 1)
                        if at + 3 < NG:
                            load_rel(act, r, k + 3)
                        if at + 2 < NG:
                            load_ea(act, r, k + 2)
                            load_windows(act, r, k + 2)
                        if at + 4 < NG:
                            act.dma_start(idx[:, k % 4], src[bass.ds(g + 4, 1)].rearrange("o p t -> (o p) t")
                                          ).then_inc(idx_in[k % 4], 16)

                    engine_turns(act, weights)

                @block.vector
                def _(dve):
                    chained = [0]

                    def link(ins):
                        chained[0] += 1
                        ins.then_inc(tables_chain, 1)
                        dve.wait_ge(tables_chain, chained[0])

                    if first:
                        dve.wait_ge(ids_made, 2)
                        nc.vector.tensor_copy(ps_ids, node_row[:]).then_inc(ids_up, 1)
                        dve.wait_ge(dst_in, 32)
                        nc.vector.tensor_reduce(ranges[:, 0:1], dstg[:], AX.X, ALU.min)
                        link(nc.vector.scalar_tensor_tensor(out=dst_masked[:], in0=dstg[:], scalar=float(N),
                                                            in1=dstg[:], op0=ALU.is_lt, op1=ALU.mult))
                        link(nc.vector.tensor_reduce(ranges[:, 2:3], dst_masked[:], AX.X, ALU.max))
                        nc.vector.tensor_tensor(ranges[:, 1:2], ranges[:, 2:3], ranges[:, 0:1],
                                                ALU.subtract).then_inc(range_up, 1)
                        dve.wait_ge(range_in, 16)
                        link(nc.vector.reduce_max(checks[:, 0:1], ranges_all[:, :, 1], AX.X))
                        link(nc.vector.tensor_scalar(checks[:, 1:2], checks[:, 0:1], float(P), None, ALU.is_lt))
                        nc.vector.tensor_scalar(base_all[:], ranges_all[:, :, 0], checks[:, 1:2], None, ALU.mult)
                        nc.vector.memset(window[:], 0.0)
                        link(nc.vector.tensor_scalar(ranges[:, 3:4], ranges[:, 0:1], checks[0:NG, 1:2], None,
                                                     ALU.mult))
                    else:
                        link(nc.vector.tensor_scalar(window[:], window[:], float(P), None, ALU.add))
                        nc.vector.tensor_scalar(base_all[:], base_all[:], 0.0, window[:], ALU.mult, ALU.add)
                        link(nc.vector.tensor_copy(ranges[:, 3:4], window[0:NG, :]))
                    nc.vector.tensor_copy(base_int[:], base_all[:])
                    nc.vector.tensor_scalar(rel_group[:], dstg[:], ranges[:, 3:4], None, ALU.subtract)
                    link(nc.vector.tensor_tensor(rel_tile[:].rearrange("p (g t) -> p g t", t=T),
                                                 dstp[:].rearrange("p (g t) -> p g t", t=T),
                                                 base_all[:].unsqueeze(2).broadcast_to([P, NG, T]),
                                                 ALU.subtract))
                    dve.sem_inc(tables_up, 1)
                    if first:
                        nc.vector.tensor_copy(steps[:, 0:1], base_all[:, 0:1])
                        nc.vector.tensor_tensor(steps[:, 1:NG], base_all[:, 1:NG], base_all[:, 0:NG - 1],
                                                ALU.subtract)
                        nc.vector.tensor_scalar(checks[:, 2:3], base_all[:, 0:1], 0.0, None, ALU.is_le)
                        nc.vector.tensor_scalar(checks[:, 3:4], base_all[:, NG - 1:NG], float(N - P), None,
                                                ALU.is_ge)
                        link(nc.vector.tensor_scalar(steps[:, NG:NG + 1], checks[:, 1:2], 0.0, None, ALU.mult))
                        link(nc.vector.reduce_max(checks[:, 4:5], steps[:], AX.X))
                        link(nc.vector.tensor_scalar(checks[:, 5:6], checks[:, 4:5], float(P), checks[:, 2:3],
                                                     ALU.is_le, ALU.mult))
                        link(nc.vector.tensor_tensor(checks[:, 6:7], checks[:, 5:6], checks[:, 3:4], ALU.mult))
                        link(nc.vector.tensor_tensor(checks[:, 7:8], checks[:, 6:7], checks[:, 1:2], ALU.mult))
                        link(nc.vector.tensor_tensor(checks[:, 7:8], checks[:, 7:8], checks[:, 1:2], ALU.add))
                        link(nc.vector.tensor_scalar(left_int[:], checks[:, 7:8], -1.0, 2.0, ALU.mult, ALU.add))
                        def remainder(n):
                            dve.wait_ge(q_hi, n + 1)
                            if n >= 2:
                                dve.wait_ge(q_up, n - 1)
                            nc.vector.scalar_tensor_tensor(
                                out=q_rest[:, n % 2],
                                in0=q_banks[n % 4][:, 0:QB * D].rearrange("p (j f) -> p j f", j=QB),
                                scalar=float(HD) ** -0.5, in1=q_parts[:, n * QB:(n + 1) * QB, 0],
                                op0=ALU.mult, op1=ALU.subtract).then_inc(q_r, 1)

                        remainder(0)
                        for n in range(NR // P // QB):
                            if n + 1 < NR // P // QB:
                                remainder(n + 1)
                            dve.wait_ge(q_mid, n + 1)
                            nc.vector.tensor_tensor(q_parts[:, n * QB:(n + 1) * QB, 2], q_rest[:, n % 2],
                                                    q_parts[:, n * QB:(n + 1) * QB, 1],
                                                    ALU.subtract).then_inc(q_up, 1)

                    def make_pick(r, k, at):
                        g = U * r + k
                        dve.wait_ge(rel_in[k % 4], 16 * lap(r, k, 4))
                        if at >= 2:
                            dve.wait_ge(q_done, g - 1)
                        nc.vector.tensor_scalar(pick[:, k % 2], rel[:, k % 4], node_id[:], None,
                                                ALU.is_equal).then_inc(pick_done, 1)

                    def make_place(r, k, at):
                        g = U * r + k
                        if at >= 2:
                            dve.wait_ge(sum_done, g - 1)
                        nc.vector.tensor_tensor(
                            place[:, k % 2], ps_ids.unsqueeze(1).broadcast_to([P, T, P]),
                            rel_tile[:, bass.ds(g * T, T)].unsqueeze(2).broadcast_to([P, T, P]),
                            ALU.is_equal).then_inc(place_done, 1)

                    def mean_step(n, r, k, at):
                        if not first or not 0 <= at < NG:
                            return
                        g = U * r + k
                        s = k % 2
                        if n == 0:
                            dve.wait_ge(merge_done, g + 1)
                            ins = nc.vector.tensor_scalar(rz[:, 0], accw[:, s, D:ML], EPS_Z, None, ALU.add)
                        else:
                            if n == 3:
                                dve.wait_ge(xwin_in[k % 4], 16 * lap(r, k, 4))
                            dve.wait_ge(mean_steps, MEAN_STEPS * g + n)
                        if n == 1:
                            ins = nc.vector.reciprocal(rz[:, 1], rz[:, 0])
                        if n == 2:
                            ins = nc.vector.tensor_tensor(hw[:].rearrange("p (h d) -> p h d", h=H),
                                                          accw[:, s, 0:D].rearrange("p (h d) -> p h d", h=H),
                                                          rz[:, 1].unsqueeze(2).broadcast_to([P, H, HD]), ALU.mult)
                        if n == 3:
                            ins = nc.vector.tensor_tensor(yw[:, s], hw[:], xwin[:, k % 4], ALU.add)
                        if n == 4:
                            ins = nc.vector.bn_stats(bn[:], yw[:, s])
                        ins.then_inc(mean_steps, 1)

                    def out_step(n, r, k, at):
                        if not first or not 0 <= at < NG:
                            return
                        g = U * r + k
                        s = k % 2
                        if n == 0:
                            if at >= 1:
                                dve.wait_ge(fin_done, g)
                            dve.wait_ge(mean_steps, MEAN_STEPS * (g + 1))
                            dve.sem_inc(out_steps, 1)
                            ins = nc.vector.bn_aggr(stat[:, 0:2], bn[:])
                        if n == 1:
                            dve.wait_ge(out_steps, OUT_STEPS * g + 2)
                            ins = nc.vector.tensor_scalar(stat[:, 2:3], stat[:, 1:2], EPS_LN, None, ALU.add)
                        if n == 2:
                            dve.wait_ge(out_steps, OUT_STEPS * g + 3)
                            dve.wait_ge(root_done, g + 1)
                            ins = nc.vector.scalar_tensor_tensor(
                                out=stat[:, 5:6], in0=stat[:, 4:5], scalar=stat[:, 2:3], in1=stat[:, 4:5],
                                op0=ALU.mult, op1=ALU.mult)
                        if n == 3:
                            dve.wait_ge(out_steps, OUT_STEPS * g + 4)
                            ins = nc.vector.tensor_scalar(stat[:, 6:7], stat[:, 5:6], -0.5, 1.5, ALU.mult, ALU.add)
                        if n == 4:
                            dve.wait_ge(out_steps, OUT_STEPS * g + 5)
                            ins = nc.vector.tensor_tensor(stat[:, 7:8], stat[:, 4:5], stat[:, 6:7], ALU.mult)
                        if n < 5:
                            ins.then_inc(out_steps, 1)
                        else:
                            if at >= 2:
                                dve.wait_ge(out_out[s], 16 * lap(r, k - 2, 2))
                            dve.wait_ge(out_steps, OUT_STEPS * (g + 1))
                            nc.vector.tensor_scalar(outw[:, s], yw[:, s], stat[:, 0:1], stat[:, 7:8],
                                                    ALU.subtract, ALU.mult).then_inc(fin_done, 1)

                    def arithmetic(r, k, at):
                        g = U * r + k
                        s = k % 2
                        last_window, window_before = (r, k - 1, at - 1), (r, k - 2, at - 2)
                        if at < NG:
                            gathered = 16 * T * lap(r, k, 4)
                            if at == NG - 1:
                                gathered -= 16 * (T - LAST_TILES)
                            dve.wait_ge(q_done, g + 1)
                            if at >= 1:
                                dve.wait_ge(qke_done, g)
                            dve.wait_ge(kv_in[k % 4], gathered)
                            nc.vector.tensor_tensor(
                                qk[:].rearrange("p (b t) d -> p b t d", b=2),
                                psQ[:, :, 0:4 * D].rearrange("p b (t d) -> p b t d", t=4),
                                kv[:, k % 4, :, 0:D].rearrange("p (b t) d -> p b t d", b=2),
                                ALU.mult).then_inc(qk_done, 1)
                        out_step(0, *window_before)
                        if at < NG:
                            dve.wait_ge(e_done, g + 1)
                            if at >= 1:
                                dve.wait_ge(logit_done, g)
                            dve.wait_ge(qk_done, g + 1)
                            nc.vector.tensor_tensor(
                                qke[:].rearrange("p (b t) d -> p b t d", b=2),
                                psE[:, :, 0:4 * D].rearrange("p b (t d) -> p b t d", t=4),
                                qk[:].rearrange("p (b t) d -> p b t d", b=2), ALU.mult).then_inc(qke_done, 1)
                        out_step(1, *window_before)
                        if 1 <= at <= NG:
                            dve.wait_ge(accw_in[1 - s], 16 * lap(r, k - 1, 2))
                            dve.wait_ge(sum_done, g)
                            nc.vector.tensor_tensor(accw[:, 1 - s], psA[:, 1 - s, 0:ML], accw[:, 1 - s],
                                                    ALU.add).then_inc(merge_done, 1)
                        if at < NG:
                            if at >= 1:
                                dve.wait_ge(clip_done, g)
                            dve.wait_ge(qke_done, g + 1)
                            nc.vector.tensor_reduce(logit[:], qke[:].rearrange("p t (h d) -> p (t h) d", h=H),
                                                    AX.X, ALU.add).then_inc(logit_done, 1)
                        mean_step(0, *last_window)
                        if at < NG:
                            if at >= 2:
                                dve.wait_ge(wt_done, g - 1)
                            dve.wait_ge(logit_done, g + 1)
                            nc.vector.tensor_scalar(clipped[:, s], logit[:], -5.0, 5.0, ALU.max,
                                                    ALU.min).then_inc(clip_done, 1)
                        mean_step(1, *last_window)
                        if at + 1 < NG:
                            make_place(r, k + 1, at + 1)
                        mean_step(2, *last_window)
                        out_step(2, *window_before)
                        if at < NG:
                            if at >= 2:
                                dve.wait_ge(sum_done, g - 1)
                            dve.wait_ge(exp_done, g + 1)
                            nc.vector.tensor_tensor(
                                msg[:, s, :, 0:D].rearrange("p t (h d) -> p t h d", h=H),
                                kv[:, k % 4, :, D:2 * D].rearrange("p t (h d) -> p t h d", h=H),
                                ps_wt.rearrange("p (t h) -> p t h", t=T).unsqueeze(3)
                                .broadcast_to([P, T, H, HD]), ALU.mult).then_inc(msg_done, 1)
                        mean_step(3, *last_window)
                        out_step(3, *window_before)
                        if at + 2 < NG:
                            make_pick(r, k + 2, at + 2)
                        mean_step(4, *last_window)
                        out_step(4, *window_before)
                        out_step(5, *window_before)

                    for g in range(2):
                        make_pick(0, g, g)
                    make_place(0, 0, 0)
                    engine_turns(dve, arithmetic)

        def next_pass():
            nc.all_engine_barrier(sems_to_clear=range(sems[0].num, sems[-1].num + 1))

        def all_outputs():
            hsum = zeros[:, 0:OT * ML].rearrange("p (t f) -> p t f", t=OT)
            xr = kv_stage[:].rearrange("p t f -> p (t f)")[:, 0:OT * D].rearrange("p (t f) -> p t f", t=OT)
            y = xt[:, 0:OT * D].rearrange("p (t f) -> p t f", t=OT)
            y2 = kv_stage[:].rearrange("p t f -> p (t f)")[:, OT * D:2 * OT * D].rearrange("p (t f) -> p t f", t=OT)
            rzs = q_parts[:].rearrange("p t s d -> p (t s d)")[:, 0:2 * OT * H].bitcast(f32)
            rzs = rzs.rearrange("p (t h) -> p t h", t=OT)
            st = dst_stats
            with nc.Block() as block:
                @block.sync
                def _(sp):
                    sp.dma_start(hsum, acc_table[0:NW * P, :].rearrange("(p t) f -> p t f", p=P)).then_inc(w_in, 16)
                    sp.dma_start(xr, xrows[0:NW * P, :].rearrange("(p t) f -> p t f", p=P)).then_inc(we_in, 16)
                    sp.wait_ge(fin_done, 1)
                    sp.dma_start(out[0:NW * P, :].rearrange("(p t) f -> p t f", p=P), y).then_inc(kv_out, 16)
                    sp.wait_ge(kv_out, 16)

                @block.scalar
                def _(act):
                    act.wait_ge(log_done, 1)
                    nc.scalar.activation(y2, y, ACT.Square).then_inc(root_done, 1)
                    act.wait_ge(log_done, 2)
                    nc.scalar.activation(st[:, 3], st[:, 2], ACT.Sqrt).then_inc(root_done, 1)

                @block.vector
                def _(dve):
                    chained = [0]

                    def link(ins):
                        chained[0] += 1
                        ins.then_inc(tables_chain, 1)
                        dve.wait_ge(tables_chain, chained[0])

                    dve.wait_ge(w_in, 16)
                    link(nc.vector.tensor_scalar(rzs, hsum[:, :, D:ML], EPS_Z, None, ALU.add))
                    link(nc.vector.reciprocal(rzs, rzs))
                    link(nc.vector.tensor_tensor(y.rearrange("p t (h d) -> p t h d", h=H),
                                                 hsum[:, :, 0:D].rearrange("p t (h d) -> p t h d", h=H),
                                                 rzs.unsqueeze(3).broadcast_to([P, OT, H, HD]), ALU.mult))
                    dve.wait_ge(we_in, 16)
                    link(nc.vector.tensor_tensor(y, y, xr, ALU.add))
                    link(nc.vector.reduce_sum(st[:, 0], y, AX.X))
                    link(nc.vector.tensor_scalar(st[:, 1], st[:, 0], 1.0 / D, None, ALU.mult))
                    nc.vector.tensor_tensor(y, y, st[:, 1].unsqueeze(2).broadcast_to([P, OT, D]),
                                            ALU.subtract).then_inc(log_done, 1)
                    dve.wait_ge(root_done, 1)
                    link(nc.vector.reduce_sum(st[:, 0], y2, AX.X))
                    nc.vector.tensor_scalar(st[:, 2], st[:, 0], 1.0 / D, EPS_LN, ALU.mult, ALU.add
                                            ).then_inc(log_done, 1)
                    dve.wait_ge(root_done, 2)
                    link(nc.vector.reciprocal(st[:, 4], st[:, 3]))
                    nc.vector.tensor_tensor(y, y, st[:, 4].unsqueeze(2).broadcast_to([P, OT, D]),
                                            ALU.mult).then_inc(fin_done, 1)

        dst_stats = sb("dst_stats", [P, 5, OT], f32)
        edge_pass(True)
        left = nc.values_load(left_int[0:1, 0:1], min_val=0, max_val=2)
        with nc.If(left > 0):
            next_pass()
            with nc.If(left > 1):
                with nc.Fori(1, NW):
                    edge_pass(False)
                    next_pass()
            all_outputs()


def kernel(x, src, dst, edge_attr_96, L0_gnn_Wq, L0_gnn_bq, L0_gnn_Wk, L0_gnn_bk, L0_gnn_We, L0_gnn_be,
           L0_gnn_Wv, L0_gnn_bv):
    import numpy as np
    import concourse.bacc as bacc
    from concourse.bass_utils import run_bass_kernel_spmd

    x, src, dst, ea = (np.asarray(a) for a in (x, src, dst, edge_attr_96))
    wq, bq, wk, bk, we, be, wv, bv = (np.asarray(a) for a in (
        L0_gnn_Wq, L0_gnn_bq, L0_gnn_Wk, L0_gnn_bk, L0_gnn_We, L0_gnn_be, L0_gnn_Wv, L0_gnn_bv))
    xT = np.zeros((D, NR), x.dtype)
    xT[:, :N] = x.T
    xrows = np.zeros((NR, D), x.dtype)
    xrows[:N] = x
    src_pad = np.zeros(NG * GE, src.dtype)
    src_pad[:E] = src
    dst_pad = np.full(NG * GE, N, dst.dtype)
    dst_pad[:E] = dst
    eaT = np.zeros((NG * GE, D), ea.dtype)
    eaT[:E] = ea
    arrays = {
        "xT": xT,
        "ones": np.ones((1, NR), x.dtype),
        "xrows": xrows,
        "src": np.ascontiguousarray(src_pad.reshape(NG, T, P).transpose(0, 2, 1)),
        "dst_group": dst_pad.reshape(NG, GE),
        "dst_tile": np.ascontiguousarray(dst_pad.reshape(NG * T, P).T),
        "eaT": np.ascontiguousarray(eaT.reshape(NG, GE, D).transpose(0, 2, 1)),
        "w_node": np.concatenate([np.concatenate([wk, wv, wq], 1), np.concatenate([bk, bv, bq])[None]], 0),
        "w_edge": np.concatenate([we, be[None]], 0),
    }
    nc = bacc.Bacc("TRN2", target_bir_lowering=False, num_devices=1)
    args = [nc.dram_tensor(n, a.shape, mybir.dt.from_np(a.dtype), kind="ExternalInput").ap()
            for n, a in arrays.items()]
    out = nc.dram_tensor("out", (NR, D), mybir.dt.float32, kind="ExternalOutput").ap()
    gnn_program(nc, *args, out)
    r = run_bass_kernel_spmd(nc, [arrays], core_ids=[0])
    return r.results[0]["out"][:N]
```

```python
import concourse.bass as bass
from concourse import mybir
from contextlib import ExitStack

P = 128
N = 6250
E = 100000
D = 96
H = 8
HD = D // H
DA = D + 1
T = 8
GE = T * P
NG = -(-E // GE)
LAST_TILES = 2 * -(-(E - (NG - 1) * GE) // (2 * P))
NW = -(-N // P)
NR = (NW + 1) * P
ML = D + H
EPS_Z = 1e-6
EPS_LN = 1e-5
U = 8
TURNS = (NG - U) // U
XG = 4
KV_CHUNKS = (4, 6, 10, 10, 8, 6, 4, 2)
Q_CHUNKS = (10, 10, 10, 10, 5, 5)
OT = NW
QB = 5
ZT = 10
MEAN_STEPS, OUT_STEPS = 5, 6


def chunked(sizes):
    return [(sum(sizes[:c]), size) for c, size in enumerate(sizes)]


def lap(r, k, ring):
    return (U // ring) * r + k // ring + 1


def gnn_program(nc, xT, ones, xrows, src, dst_group, dst_tile, eaT, w_node, w_edge, out):
    f32, bf16, i32 = mybir.dt.float32, mybir.dt.bfloat16, mybir.dt.int32
    ALU, ACT, AX = mybir.AluOpType, mybir.ActivationFunctionType, mybir.AxisListType

    kv_table = nc.dram_tensor("kv_table", (NR, 2 * D), f32, kind="Internal").ap()
    q_table = nc.dram_tensor("q_table", (NR, 3 * D), bf16, kind="Internal").ap()
    rel_table = nc.dram_tensor("rel_table", (NG, GE), bf16, kind="Internal").ap()
    range_table = nc.dram_tensor("range_table", (NG, 2), f32, kind="Internal").ap()
    acc_table = nc.dram_tensor("acc_table", (NR, ML), f32, kind="Internal").ap()

    ctx = ExitStack()
    with ctx:
        def sb(name, shape, dt):
            return ctx.enter_context(nc.sbuf_tensor(name, shape, dt))

        def ps(name, shape, dt):
            return ctx.enter_context(nc.psum_tensor(name, shape, dt))

        sems = []

        def sem(name):
            sems.append(ctx.enter_context(nc.semaphore(name)))
            return sems[-1]

        wn = sb("wn", [DA, 3 * D], f32)
        we = sb("we", [DA, D], f32)
        xt = sb("xt", [P, NR], f32)
        kv = sb("kv", [P, U, T, 2 * D], f32)
        kv_stage = kv[:].rearrange("p s t f -> p (s t) f")[:, 0:NR // P]
        q_parts = sb("q_parts", [P, NR // P, 3, D], bf16)
        q_rest = sb("q_rest", [P, 2, QB, D], f32)
        zeros = sb("zeros", [P, ZT * ML], f32)
        xg = sb("xg", [P, XG, T, D], f32)
        identity = sb("identity", [P, P], f32)
        dstg = sb("dstg", [NG, GE], i32)
        dstp = sb("dstp", [P, NG * T], i32)
        dst_masked = sb("dst_masked", [NG, GE], f32)
        ranges = sb("ranges", [NG, 4], f32)
        ranges_all = sb("ranges_all", [P, NG, 2], f32)
        steps = sb("steps", [P, NG + 1], f32)
        checks = sb("checks", [P, 8], f32)
        base_all = sb("base_all", [P, NG], f32)
        base_int = sb("base_int", [P, NG], i32)
        left_int = sb("left_int", [P, 1], i32)
        window = sb("window", [P, 1], f32)
        rel_group = sb("rel_group", [NG, GE], bf16)
        rel_tile = sb("rel_tile", [P, NG * T], bf16)
        node_id = sb("node_id", [P, 1], f32)
        node_row = sb("node_row", [P, P], f32)
        idx = sb("idx", [P, U, T], i32)
        ea = sb("ea", [DA, 2, GE], f32)
        rel = sb("rel", [P, 4, GE], bf16)
        qwin = sb("qwin", [P, 2, 3, D], bf16)
        xwin = sb("xwin", [P, 4, D], f32)
        pick = sb("pick", [P, 2, GE], bf16)
        place = sb("place", [P, 2, T, P], f32)
        qk = sb("qk", [P, T, D], f32)
        qke = sb("qke", [P, T, D], f32)
        logit = sb("logit", [P, T * H], f32)
        clipped = sb("clipped", [P, 2, T * H], f32)
        msg = sb("msg", [P, 2, T, ML], f32)
        accw = sb("accw", [P, 2, ML], f32)
        rz = sb("rz", [P, 2, H], f32)
        hw = sb("hw", [P, D], f32)
        yw = sb("yw", [P, 2, D], f32)
        outw = sb("outw", [P, 2, D], f32)
        bn = sb("bn", [P, 6], f32)
        stat = sb("stat", [P, 8], f32)
        psE = ps("psE", [P, 2, 512], f32)
        psQ = ps("psQ", [P, 2, 512], f32)
        psA = ps("psA", [P, 2, 512], f32)
        psI = ps("psI", [P, 512], f32)
        psW = ps("psW", [P, 512], f32)
        ps_ids = psI[:, 0:P]
        ps_wt = psW[:, 0:T * H]
        kv_banks = [psE[:, 0], psE[:, 1], psA[:, 0], psA[:, 1]]
        turn_banks, conv_banks = [psE[:, 1], psA[:, 1], psQ[:, 0], psQ[:, 1]], [psA[:, 0], psW[:, :]]
        q_banks = [psQ[:, 0], psQ[:, 1], psW[:, :], psE[:, 0]]

        w_in, we_in, dst_in, ones_in = sem("w_in"), sem("we_in"), sem("dst_in"), sem("ones_in")
        xt_in = [sem(f"xt_in{c}") for c in range(len(KV_CHUNKS))]
        ids_made, ids_up, zero_set = sem("ids_made"), sem("ids_up"), sem("zero_set")
        kv_mm, kv_up, kv_out = sem("kv_mm"), sem("kv_up"), sem("kv_out")
        q_mm, q_hi, q_r, q_mid, q_up = sem("q_mm"), sem("q_hi"), sem("q_r"), sem("q_mid"), sem("q_up")
        q_out = sem("q_out")
        acc_zeroed = sem("acc_zeroed")
        range_up, range_out, range_in = sem("range_up"), sem("range_out"), sem("range_in")
        tables_chain, tables_up, rel_out = sem("tables_chain"), sem("tables_up"), sem("rel_out")

        idx_in = [sem(f"idx_in{i}") for i in range(U)]
        xg_in = [sem(f"xg_in{i}") for i in range(XG)]
        turned, turned_up, conv_mm, conv_up = sem("turned"), sem("turned_up"), sem("conv_mm"), sem("conv_up")
        kv_in = [sem(f"kv_in{i}") for i in range(U)]
        ea_in = [sem(f"ea_in{i}") for i in range(2)]
        rel_in = [sem(f"rel_in{i}") for i in range(4)]
        qwin_in = [sem(f"qwin_in{i}") for i in range(2)]
        xwin_in = [sem(f"xwin_in{i}") for i in range(4)]
        accw_in = [sem(f"accw_in{i}") for i in range(2)]
        accw_out = [sem(f"accw_out{i}") for i in range(2)]
        out_out = [sem(f"out_out{i}") for i in range(2)]
        e_done, q_done, sum_done = sem("e_done"), sem("q_done"), sem("sum_done")
        pick_done, place_done = sem("pick_done"), sem("place_done")
        qk_done, qke_done, logit_done = sem("qk_done"), sem("qke_done"), sem("logit_done")
        clip_done, msg_done, merge_done = sem("clip_done"), sem("msg_done"), sem("merge_done")
        exp_done, wt_done = sem("exp_done"), sem("wt_done")
        mean_steps, out_steps = sem("mean_steps"), sem("out_steps")
        log_done, root_done, fin_done = sem("log_done"), sem("root_done"), sem("fin_done")
        gathers_begun, outputs_begun = sem("gathers_begun"), sem("outputs_begun")

        def tiles(at):
            return LAST_TILES if at == NG - 1 else T

        def engine_turns(eng, body):
            for k in range(U):
                body(0, k, k)
            with eng.Fori(1, TURNS) as r:
                for k in range(U):
                    body(r, k, U + k)
            for at in range(TURNS * U, NG + 2):
                body(at // U, at % U, at)

        def edge_pass(first):
            def load_rel(eng, r, k):
                eng.dma_start(rel[:, k % 4], rel_table[bass.ds(U * r + k, 1), :].broadcast_to([P, GE])
                              ).then_inc(rel_in[k % 4], 16)

            def load_idx(eng, g):
                eng.dma_start(idx[:, g % U], src[g]).then_inc(idx_in[g % U], 16)

            def load_ea(eng, r, k):
                eng.dma_start(ea[0:D, k % 2], eaT[bass.ds(U * r + k, 1)].rearrange("o d e -> (o d) e")
                              ).then_inc(ea_in[k % 2], 16)

            def load_windows(eng, r, k):
                base = eng.value_load(base_int[0:1, bass.ds(U * r + k, 1)], min_val=0, max_val=NR - P)
                eng.dma_start(qwin[:, k % 2].rearrange("p s d -> p (s d)"), q_table[bass.ds(base, P), :]
                              ).then_inc(qwin_in[k % 2], 16)
                if first:
                    eng.dma_start(xwin[:, k % 4], xrows[bass.ds(base, P), :]).then_inc(xwin_in[k % 4], 16)

            with nc.Block() as block:

                @block.sync
                def _(sp):
                    if first:
                        sp.dma_start(wn[:], w_node).then_inc(w_in, 16)
                        for c, (tile, size) in enumerate(chunked(KV_CHUNKS)):
                            cols = slice(tile * P, (tile + size) * P)
                            sp.dma_start(xt[0:D, cols], xT[:, cols]).then_inc(xt_in[c], 16)
                            if c == 0:
                                sp.dma_start(xt[D:DA, :], ones).then_inc(ones_in, 16)
                            if c == 1:
                                sp.dma_start(dstg[:], dst_group).then_inc(dst_in, 16)
                                sp.dma_start(dstp[:], dst_tile).then_inc(dst_in, 16)
                        sp.dma_start(we[:], w_edge).then_inc(we_in, 16)
                        for s in range(2):
                            sp.dma_start(ea[D:DA, s], ones[:, 0:GE]).then_inc(we_in, 16)
                        for c, (tile, size) in enumerate(chunked(KV_CHUNKS)):
                            sp.wait_ge(kv_up, (tile + size) // 2)
                            sp.dma_start(kv_table[tile * P:(tile + size) * P, :].rearrange("(p t) f -> p t f", p=P),
                                         kv_stage[:, tile:tile + size]).then_inc(kv_out, 16)
                            if c == 0:
                                sp.wait_ge(range_up, 1)
                                sp.dma_start(range_table, ranges[:, 0:2]).then_inc(range_out, 16)
                            if c == 2:
                                sp.wait_ge(range_out, 16)
                                sp.dma_start(ranges_all[:].rearrange("p g c -> p (g c)"),
                                             range_table.rearrange("g c -> (g c)").unsqueeze(0)
                                             .broadcast_to([P, NG * 2])).then_inc(range_in, 16)
                    sp.wait_ge(tables_up, 1)
                    sp.dma_start(rel_table, rel_group[:]).then_inc(rel_out, 16)

                    def first_loads():
                        sp.wait_ge(rel_out, 16)
                        for g in range(3):
                            load_rel(sp, 0, g)
                        for g in range(2):
                            load_ea(sp, 0, g)

                    if first:
                        for c, (tile, size) in enumerate(chunked(Q_CHUNKS)):
                            if c == 2:
                                first_loads()
                            sp.wait_ge(q_up, (tile + size) // QB)
                            sp.dma_start(q_table[tile * P:(tile + size) * P, :].rearrange("(p t) f -> p t f", p=P),
                                         q_parts[:, tile:tile + size].rearrange("p t s d -> p t (s d)")
                                         ).then_inc(q_out, 16)
                        sp.wait_ge(q_out, 16 * len(Q_CHUNKS))
                    else:
                        first_loads()
                    for g in range(2):
                        load_windows(sp, 0, g)
                    if first:
                        sp.wait_ge(zero_set, 1)
                        sp.dma_start(acc_table.rearrange("(p u t) f -> p u (t f)", p=P, t=ZT),
                                     zeros[:].unsqueeze(1).broadcast_to([P, NR // P // ZT, ZT * ML])
                                     ).then_inc(acc_zeroed, 16)
                        sp.wait_ge(acc_zeroed, 16)

                    def base_of(g):
                        return sp.value_load(base_int[0:1, bass.ds(g, 1)], min_val=0, max_val=NR - P)

                    def sums(r, k, at):
                        g = U * r + k
                        s = k % 2
                        if first and at >= 2:
                            base = base_of(g - 2)
                            if at >= 3:
                                sp.wait_ge(out_out[1 - s], 16 * lap(r, k - 3, 2))
                                sp.sem_inc(outputs_begun, 1)
                            sp.wait_ge(fin_done, g - 1)
                            sp.dma_start(out[bass.ds(base, P), :], outw[:, s]).then_inc(out_out[s], 16)
                        if at < NG:
                            base = base_of(g)
                            sp.wait_ge(merge_done, g + 1)
                            sp.dma_start(acc_table[bass.ds(base, P), :], accw[:, s]).then_inc(accw_out[s], 16)
                        if at + 1 < NG:
                            base = base_of(g + 1)
                            sp.wait_ge(accw_out[s], 16 * lap(r, k, 2))
                            sp.dma_start(accw[:, 1 - s], acc_table[bass.ds(base, P), :]
                                         ).then_inc(accw_in[1 - s], 16)

                    sp.dma_start(accw[:, 0], acc_table[bass.ds(base_of(0), P), :]).then_inc(accw_in[0], 16)
                    engine_turns(sp, sums)
                    for s in range(2):
                        sp.wait_ge(accw_out[s], 16 * ((NG - s + 1) // 2))
                        if first:
                            sp.wait_ge(out_out[s], 16 * ((NG - s + 1) // 2))

                @block.gpsimd
                def _(pool):
                    if first:
                        nc.gpsimd.iota(node_id[:], pattern=[[0, 1]], base=0, channel_multiplier=1,
                                       allow_small_or_imprecise_dtypes=True).then_inc(ids_made, 1)
                        nc.gpsimd.iota(node_row[:], pattern=[[1, P]], base=0, channel_multiplier=0,
                                       allow_small_or_imprecise_dtypes=True).then_inc(ids_made, 1)

                    def gathers(r, k, at):
                        if at >= NG:
                            return
                        g = U * r + k
                        if at >= U:
                            pool.wait_ge(msg_done, g - U + 1)
                        if first and at == XG:
                            pool.wait_ge(kv_out, 16 * len(KV_CHUNKS))
                        pool.wait_ge(idx_in[k], 16 * (r + 1))
                        pool.sem_inc(gathers_begun, 1)
                        for t in range(tiles(at)):
                            sources = bass.IndirectOffsetOnAxis(ap=idx[:, k, t:t + 1], axis=0)
                            if first and at < XG:
                                pool.indirect_dma_start(xg[:, k, t], None, xrows, sources).then_inc(xg_in[k], 16)
                            else:
                                pool.indirect_dma_start(kv[:, k, t], None, kv_table, sources
                                                        ).then_inc(kv_in[k], 16)

                    engine_turns(pool, gathers)
                    for s in range(U):
                        groups = len(range(s, NG, U)) - (1 if first and s < XG else 0)
                        missing = (T - LAST_TILES) if s == (NG - 1) % U else 0
                        pool.wait_ge(kv_in[s], 16 * (T * groups - missing))
                    if first:
                        for s in range(XG):
                            pool.wait_ge(xg_in[s], 16 * T)
                    nc.gpsimd.dma_reset()

                @block.tensor
                def _(pe):
                    if first:
                        pe.wait_ge(w_in, 16)
                        pe.wait_ge(ones_in, 16)
                        for c, (tile, size) in enumerate(chunked(KV_CHUNKS)):
                            pe.wait_ge(xt_in[c], 16)
                            nodes = xt[0:DA, tile * P:(tile + size) * P].rearrange("d (p t) -> d t p", t=size)
                            for t in range(0, size, 2):
                                n = (tile + t) // 2
                                if n >= 4:
                                    pe.wait_ge(kv_up, n - 3)
                                for j in range(2):
                                    last = nc.tensor.matmul(kv_banks[n % 4][:, j * 2 * D:(j + 1) * 2 * D],
                                                            nodes[:, t + j], wn[:, 0:2 * D],
                                                            start=True, stop=True)
                                last.then_inc(kv_mm, 1)
                        pe.wait_ge(kv_up, NR // P // 2)
                        for tile, size in chunked(Q_CHUNKS):
                            nodes = xt[0:DA, tile * P:(tile + size) * P].rearrange("d (p t) -> d t p", t=size)
                            for t in range(0, size, QB):
                                n = (tile + t) // QB
                                if n >= 4:
                                    pe.wait_ge(q_r, n - 3)
                                for j in range(QB):
                                    last = nc.tensor.matmul(q_banks[n % 4][:, j * D:(j + 1) * D],
                                                            nodes[:, t + j], wn[:, 2 * D:3 * D],
                                                            start=True, stop=True)
                                last.then_inc(q_mm, 1)
                        pe.wait_ge(we_in, 48)
                        pe.wait_ge(q_r, NR // P // QB)

                    def to_edges_q(r, k, at):
                        g = U * r + k
                        pe.wait_ge(qwin_in[k % 2], 16 * lap(r, k, 2))
                        pe.wait_ge(pick_done, g + 1)
                        if at >= 1:
                            pe.wait_ge(qk_done, g)
                        for t in range(tiles(at)):
                            for s in range(3):
                                last = nc.tensor.matmul(
                                    psQ[:, t % 2, t // 2 * D:(t // 2 + 1) * D],
                                    pick[:, k % 2, t * P:(t + 1) * P], qwin[:, k % 2, s],
                                    start=(s == 0), stop=(s == 2))
                        last.then_inc(q_done, 1)

                    def to_edges_e(r, k, at):
                        g = U * r + k
                        pe.wait_ge(ea_in[k % 2], 16 * lap(r, k, 2))
                        if at >= 1:
                            pe.wait_ge(qke_done, g)
                        for t in range(tiles(at)):
                            last = nc.tensor.matmul(
                                psE[:, t % 2, t // 2 * D:(t // 2 + 1) * D],
                                ea[:, k % 2, t * P:(t + 1) * P], we[:], start=True, stop=True)
                        last.then_inc(e_done, 1)

                    def products(r, k, at):
                        g = U * r + k
                        if at + 1 < NG:
                            to_edges_q(r, k + 1, at + 1)
                            to_edges_e(r, k + 1, at + 1)
                        if at < NG:
                            s = k % 2
                            pe.wait_ge(place_done, g + 1)
                            pe.wait_ge(wt_done, g + 1)
                            if at >= 2:
                                pe.wait_ge(merge_done, g - 1)
                            pe.wait_ge(msg_done, g + 1)
                            for t in range(tiles(at)):
                                last = nc.tensor.matmul(psA[:, s, 0:ML], place[:, s, t], msg[:, s, t],
                                                        start=(t == 0), stop=(t == tiles(at) - 1))
                            last.then_inc(sum_done, 1)

                    if first:
                        pe.wait_ge(ids_up, 2)
                        for n in range(2 * XG):
                            pe.wait_ge(xg_in[n // 2], 16 * T)
                            if n >= 4:
                                pe.wait_ge(turned_up, n - 3)
                            for t in range(4):
                                last = nc.tensor.transpose(turn_banks[n % 4][0:D, t * P:(t + 1) * P],
                                                           xg[:, n // 2, 4 * (n % 2) + t], identity[:])
                            last.then_inc(turned, 1)

                        def convert(g):
                            turned_x = xt[0:DA, g * GE:(g + 1) * GE]
                            for b in range(T // 2):
                                n = T // 2 * g + b
                                if n >= 2:
                                    pe.wait_ge(conv_up, n - 1)
                                if b % 2 == 0:
                                    pe.wait_ge(turned_up, 2 * g + b // 2 + 1)
                                for j in range(2):
                                    last = nc.tensor.matmul(conv_banks[n % 2][:, j * 2 * D:(j + 1) * 2 * D],
                                                            turned_x[:, (2 * b + j) * P:(2 * b + j + 1) * P],
                                                            wn[:, 0:2 * D], start=True, stop=True)
                                last.then_inc(conv_mm, 1)

                        for g in range(XG - 1):
                            convert(g)
                        pe.wait_ge(turned_up, 2 * XG)
                    to_edges_e(0, 0, 0)
                    to_edges_q(0, 0, 0)
                    if first:
                        convert(XG - 1)
                        pe.wait_ge(conv_up, T // 2 * XG)
                    engine_turns(pe, products)

                @block.scalar
                def _(act):
                    for g in range(XG):
                        load_idx(act, g)
                    if first:
                        nc.scalar.preload_act_table_set("natural_log_exp_and_others")
                        for n in range(NR // P // 2):
                            if 8 <= n < 8 + U - XG:
                                load_idx(act, n - 8 + XG)
                            act.wait_ge(kv_mm, n + 1)
                            nc.scalar.activation(
                                kv_stage[:, 2 * n:2 * n + 2],
                                kv_banks[n % 4][:, 0:4 * D].rearrange("p (j f) -> p j f", j=2), ACT.Copy
                            ).then_inc(kv_up, 1)

                    else:
                        for g in range(XG, U):
                            load_idx(act, g)

                    if first:
                        def leading(n):
                            act.wait_ge(q_mm, n + 1)
                            nc.scalar.activation(
                                q_parts[:, n * QB:(n + 1) * QB, 0],
                                q_banks[n % 4][:, 0:QB * D].rearrange("p (j f) -> p j f", j=QB), ACT.Copy,
                                scale=float(HD) ** -0.5).then_inc(q_hi, 1)

                        leading(0)
                        for n in range(NR // P // QB):
                            if n + 1 < NR // P // QB:
                                leading(n + 1)
                            act.wait_ge(q_r, n + 1)
                            nc.scalar.activation(q_parts[:, n * QB:(n + 1) * QB, 1], q_rest[:, n % 2],
                                                 ACT.Copy).then_inc(q_mid, 1)

                    if first:
                        for n in range(2 * XG):
                            act.wait_ge(turned, n + 1)
                            nc.scalar.activation(xt[0:D, n * 4 * P:(n + 1) * 4 * P], turn_banks[n % 4][0:D, :],
                                                 ACT.Copy).then_inc(turned_up, 1)
                        for g in range(XG):
                            load_idx(act, U + g)
                        act.wait_ge(kv_out, 16 * len(KV_CHUNKS))
                        for n in range(T // 2 * XG):
                            act.wait_ge(conv_mm, n + 1)
                            nc.scalar.activation(
                                kv[:, 2 * n // T, 2 * n % T:2 * n % T + 2],
                                conv_banks[n % 2][:, 0:4 * D].rearrange("p (j f) -> p j f", j=2), ACT.Copy
                            ).then_inc(conv_up, 1)
                        act.wait_ge(conv_up, T // 2 * XG)

                    def weights(r, k, at):
                        g = U * r + k
                        if first and at >= 2:
                            act.wait_ge(out_steps, OUT_STEPS * (g - 2) + 3)
                            nc.scalar.activation(stat[:, 3:4], stat[:, 2:3], ACT.Ln).then_inc(log_done, 1)
                            act.wait_ge(log_done, g - 1)
                            nc.scalar.activation(stat[:, 4:5], stat[:, 3:4], ACT.Exp, scale=-0.5
                                                 ).then_inc(root_done, 1)
                        if at < NG:
                            act.wait_ge(clip_done, g + 1)
                            if at >= 1:
                                act.wait_ge(msg_done, g)
                            nt = tiles(at)
                            nc.scalar.activation(ps_wt[:, 0:nt * H], clipped[:, k % 2, 0:nt * H], ACT.Exp
                                                 ).then_inc(exp_done, 1)
                            if at >= 2:
                                act.wait_ge(sum_done, g - 1)
                            nc.scalar.activation(msg[:, k % 2, 0:nt, D:ML],
                                                 clipped[:, k % 2, 0:nt * H].rearrange("p (t h) -> p t h", t=nt),
                                                 ACT.Exp).then_inc(wt_done, 1)
                        if at + 3 < NG:
                            load_rel(act, r, k + 3)
                        if at + 2 < NG:
                            load_ea(act, r, k + 2)
                            load_windows(act, r, k + 2)
                        if at + U < NG and not (first and at < XG):
                            act.dma_start(idx[:, k], src[bass.ds(g + U, 1)].rearrange("o p t -> (o p) t")
                                          ).then_inc(idx_in[k], 16)

                    engine_turns(act, weights)

                @block.vector
                def _(dve):
                    chained = [0]

                    def link(ins):
                        chained[0] += 1
                        ins.then_inc(tables_chain, 1)
                        dve.wait_ge(tables_chain, chained[0])

                    if first:
                        dve.wait_ge(ids_made, 2)
                        nc.vector.tensor_copy(ps_ids, node_row[:]).then_inc(ids_up, 1)
                        nc.vector.tensor_scalar(identity[:], node_row[:], node_id[:], None, ALU.is_equal
                                                ).then_inc(ids_up, 1)
                        nc.vector.memset(zeros[:], 0.0).then_inc(zero_set, 1)
                        dve.wait_ge(dst_in, 32)
                        nc.vector.tensor_reduce(ranges[:, 0:1], dstg[:], AX.X, ALU.min)
                        link(nc.vector.scalar_tensor_tensor(out=dst_masked[:], in0=dstg[:], scalar=float(N),
                                                            in1=dstg[:], op0=ALU.is_lt, op1=ALU.mult))
                        link(nc.vector.tensor_reduce(ranges[:, 2:3], dst_masked[:], AX.X, ALU.max))
                        nc.vector.tensor_tensor(ranges[:, 1:2], ranges[:, 2:3], ranges[:, 0:1],
                                                ALU.subtract).then_inc(range_up, 1)
                        dve.wait_ge(range_in, 16)
                        link(nc.vector.reduce_max(checks[:, 0:1], ranges_all[:, :, 1], AX.X))
                        link(nc.vector.tensor_scalar(checks[:, 1:2], checks[:, 0:1], float(P), None, ALU.is_lt))
                        nc.vector.tensor_scalar(base_all[:], ranges_all[:, :, 0], checks[:, 1:2], None, ALU.mult)
                        nc.vector.memset(window[:], 0.0)
                        link(nc.vector.tensor_scalar(ranges[:, 3:4], ranges[:, 0:1], checks[0:NG, 1:2], None,
                                                     ALU.mult))
                    else:
                        link(nc.vector.tensor_scalar(window[:], window[:], float(P), None, ALU.add))
                        nc.vector.tensor_scalar(base_all[:], base_all[:], 0.0, window[:], ALU.mult, ALU.add)
                        link(nc.vector.tensor_copy(ranges[:, 3:4], window[0:NG, :]))
                    nc.vector.tensor_copy(base_int[:], base_all[:])
                    nc.vector.tensor_scalar(rel_group[:], dstg[:], ranges[:, 3:4], None, ALU.subtract)
                    link(nc.vector.tensor_tensor(rel_tile[:].rearrange("p (g t) -> p g t", t=T),
                                                 dstp[:].rearrange("p (g t) -> p g t", t=T),
                                                 base_all[:].unsqueeze(2).broadcast_to([P, NG, T]),
                                                 ALU.subtract))
                    dve.sem_inc(tables_up, 1)
                    if first:
                        nc.vector.tensor_copy(steps[:, 0:1], base_all[:, 0:1])
                        nc.vector.tensor_tensor(steps[:, 1:NG], base_all[:, 1:NG], base_all[:, 0:NG - 1],
                                                ALU.subtract)
                        nc.vector.tensor_scalar(checks[:, 2:3], base_all[:, 0:1], 0.0, None, ALU.is_le)
                        nc.vector.tensor_scalar(checks[:, 3:4], base_all[:, NG - 1:NG], float(N - P), None,
                                                ALU.is_ge)
                        link(nc.vector.tensor_scalar(steps[:, NG:NG + 1], checks[:, 1:2], 0.0, None, ALU.mult))
                        link(nc.vector.reduce_max(checks[:, 4:5], steps[:], AX.X))
                        link(nc.vector.tensor_scalar(checks[:, 5:6], checks[:, 4:5], float(P), checks[:, 2:3],
                                                     ALU.is_le, ALU.mult))
                        link(nc.vector.tensor_tensor(checks[:, 6:7], checks[:, 5:6], checks[:, 3:4], ALU.mult))
                        link(nc.vector.tensor_tensor(checks[:, 7:8], checks[:, 6:7], checks[:, 1:2], ALU.mult))
                        link(nc.vector.tensor_tensor(checks[:, 7:8], checks[:, 7:8], checks[:, 1:2], ALU.add))
                        link(nc.vector.tensor_scalar(left_int[:], checks[:, 7:8], -1.0, 2.0, ALU.mult, ALU.add))

                        def remainder(n):
                            dve.wait_ge(q_hi, n + 1)
                            if n >= 2:
                                dve.wait_ge(q_up, n - 1)
                            nc.vector.scalar_tensor_tensor(
                                out=q_rest[:, n % 2],
                                in0=q_banks[n % 4][:, 0:QB * D].rearrange("p (j f) -> p j f", j=QB),
                                scalar=float(HD) ** -0.5, in1=q_parts[:, n * QB:(n + 1) * QB, 0],
                                op0=ALU.mult, op1=ALU.subtract).then_inc(q_r, 1)

                        remainder(0)
                        for n in range(NR // P // QB):
                            if n + 1 < NR // P // QB:
                                remainder(n + 1)
                            dve.wait_ge(q_mid, n + 1)
                            nc.vector.tensor_tensor(q_parts[:, n * QB:(n + 1) * QB, 2], q_rest[:, n % 2],
                                                    q_parts[:, n * QB:(n + 1) * QB, 1],
                                                    ALU.subtract).then_inc(q_up, 1)

                    def make_pick(r, k, at):
                        g = U * r + k
                        dve.wait_ge(rel_in[k % 4], 16 * lap(r, k, 4))
                        if at >= 2:
                            dve.wait_ge(q_done, g - 1)
                        nc.vector.tensor_scalar(pick[:, k % 2], rel[:, k % 4], node_id[:], None,
                                                ALU.is_equal).then_inc(pick_done, 1)

                    def make_place(r, k, at):
                        g = U * r + k
                        if at >= 2:
                            dve.wait_ge(sum_done, g - 1)
                        nc.vector.tensor_tensor(
                            place[:, k % 2], ps_ids.unsqueeze(1).broadcast_to([P, T, P]),
                            rel_tile[:, bass.ds(g * T, T)].unsqueeze(2).broadcast_to([P, T, P]),
                            ALU.is_equal).then_inc(place_done, 1)

                    def merge(r, k, at):
                        s = k % 2
                        dve.wait_ge(accw_in[s], 16 * lap(r, k, 2))
                        dve.wait_ge(sum_done, U * r + k + 1)
                        nc.vector.tensor_tensor(accw[:, s], psA[:, s, 0:ML], accw[:, s],
                                                ALU.add).then_inc(merge_done, 1)

                    def mean_step(n, r, k, at):
                        if not first or not 0 <= at < NG:
                            return
                        g = U * r + k
                        s = k % 2
                        if n == 0:
                            dve.wait_ge(merge_done, g + 1)
                            ins = nc.vector.tensor_scalar(rz[:, 0], accw[:, s, D:ML], EPS_Z, None, ALU.add)
                        else:
                            if n == 3:
                                dve.wait_ge(xwin_in[k % 4], 16 * lap(r, k, 4))
                            dve.wait_ge(mean_steps, MEAN_STEPS * g + n)
                        if n == 1:
                            ins = nc.vector.reciprocal(rz[:, 1], rz[:, 0])
                        if n == 2:
                            ins = nc.vector.tensor_tensor(hw[:].rearrange("p (h d) -> p h d", h=H),
                                                          accw[:, s, 0:D].rearrange("p (h d) -> p h d", h=H),
                                                          rz[:, 1].unsqueeze(2).broadcast_to([P, H, HD]), ALU.mult)
                        if n == 3:
                            ins = nc.vector.tensor_tensor(yw[:, s], hw[:], xwin[:, k % 4], ALU.add)
                        if n == 4:
                            ins = nc.vector.bn_stats(bn[:], yw[:, s])
                        ins.then_inc(mean_steps, 1)

                    def out_step(n, r, k, at):
                        if not first or not 0 <= at < NG:
                            return
                        g = U * r + k
                        s = k % 2
                        if n == 0:
                            if at >= 1:
                                dve.wait_ge(fin_done, g)
                            dve.wait_ge(mean_steps, MEAN_STEPS * (g + 1))
                            dve.sem_inc(out_steps, 1)
                            ins = nc.vector.bn_aggr(stat[:, 0:2], bn[:])
                        if n == 1:
                            dve.wait_ge(out_steps, OUT_STEPS * g + 2)
                            ins = nc.vector.tensor_scalar(stat[:, 2:3], stat[:, 1:2], EPS_LN, None, ALU.add)
                        if n == 2:
                            dve.wait_ge(out_steps, OUT_STEPS * g + 3)
                            dve.wait_ge(root_done, g + 1)
                            ins = nc.vector.scalar_tensor_tensor(
                                out=stat[:, 5:6], in0=stat[:, 4:5], scalar=stat[:, 2:3], in1=stat[:, 4:5],
                                op0=ALU.mult, op1=ALU.mult)
                        if n == 3:
                            dve.wait_ge(out_steps, OUT_STEPS * g + 4)
                            ins = nc.vector.tensor_scalar(stat[:, 6:7], stat[:, 5:6], -0.5, 1.5, ALU.mult, ALU.add)
                        if n == 4:
                            dve.wait_ge(out_steps, OUT_STEPS * g + 5)
                            ins = nc.vector.tensor_tensor(stat[:, 7:8], stat[:, 4:5], stat[:, 6:7], ALU.mult)
                        if n < 5:
                            ins.then_inc(out_steps, 1)
                        else:
                            if at >= 2:
                                dve.wait_ge(out_out[s], 16 * lap(r, k - 2, 2))
                            dve.wait_ge(out_steps, OUT_STEPS * (g + 1))
                            nc.vector.tensor_scalar(outw[:, s], yw[:, s], stat[:, 0:1], stat[:, 7:8],
                                                    ALU.subtract, ALU.mult).then_inc(fin_done, 1)

                    def arithmetic(r, k, at):
                        g = U * r + k
                        s = k % 2
                        nt = tiles(at)
                        last_window, window_before = (r, k - 1, at - 1), (r, k - 2, at - 2)
                        if at == NG:
                            merge(*last_window)
                            for n in range(MEAN_STEPS):
                                mean_step(n, *last_window)
                                if n + 2 < OUT_STEPS:
                                    out_step(n + 2, *window_before)
                            return
                        if at == NG + 1:
                            for n in range(OUT_STEPS):
                                out_step(n, *window_before)
                            return

                        def between(*steps_here):
                            for step, n, window_of in steps_here:
                                if at < NG - 1 or step == out_step:
                                    step(n, *window_of)

                        dve.wait_ge(q_done, g + 1)
                        if at >= 1:
                            dve.wait_ge(qke_done, g)
                        if first and at < XG:
                            dve.wait_ge(conv_up, T // 2 * (k + 1))
                        else:
                            fills = r if first and k < XG else r + 1
                            dve.wait_ge(kv_in[k], 16 * (T * fills - (T - nt)))
                        by_bank = dict(b=2, t=nt // 2)
                        nc.vector.tensor_tensor(
                            qk[:, 0:nt].rearrange("p (t b) d -> p b t d", **by_bank),
                            psQ[:, :, 0:nt // 2 * D].rearrange("p b (t d) -> p b t d", d=D),
                            kv[:, k, 0:nt, 0:D].rearrange("p (t b) d -> p b t d", **by_bank),
                            ALU.mult).then_inc(qk_done, 1)
                        between((out_step, 0, window_before))
                        dve.wait_ge(e_done, g + 1)
                        if at >= 1:
                            dve.wait_ge(logit_done, g)
                        dve.wait_ge(qk_done, g + 1)
                        nc.vector.tensor_tensor(
                            qke[:, 0:nt].rearrange("p (t b) d -> p b t d", **by_bank),
                            psE[:, :, 0:nt // 2 * D].rearrange("p b (t d) -> p b t d", d=D),
                            qk[:, 0:nt].rearrange("p (t b) d -> p b t d", **by_bank),
                            ALU.mult).then_inc(qke_done, 1)
                        between((out_step, 1, window_before))
                        if at >= 1:
                            merge(*last_window)
                            dve.wait_ge(clip_done, g)
                        dve.wait_ge(qke_done, g + 1)
                        nc.vector.tensor_reduce(logit[:, 0:nt * H],
                                                qke[:, 0:nt].rearrange("p t (h d) -> p (t h) d", h=H), AX.X, ALU.add).then_inc(logit_done, 1)
                        between((mean_step, 0, last_window))
                        if at >= 2:
                            dve.wait_ge(wt_done, g - 1)
                        dve.wait_ge(logit_done, g + 1)
                        nc.vector.tensor_scalar(clipped[:, s, 0:nt * H], logit[:, 0:nt * H], -5.0, 5.0, ALU.max,
                                                ALU.min).then_inc(clip_done, 1)
                        between((mean_step, 1, last_window))
                        if at + 1 < NG:
                            make_place(r, k + 1, at + 1)
                        between((mean_step, 2, last_window), (out_step, 2, window_before))
                        if at >= 2:
                            dve.wait_ge(sum_done, g - 1)
                        dve.wait_ge(exp_done, g + 1)
                        nc.vector.tensor_tensor(
                            msg[:, s, 0:nt, 0:D].rearrange("p t (h d) -> p t h d", h=H),
                            kv[:, k, 0:nt, D:2 * D].rearrange("p t (h d) -> p t h d", h=H),
                            ps_wt[:, 0:nt * H].rearrange("p (t h) -> p t h", t=nt).unsqueeze(3)
                            .broadcast_to([P, nt, H, HD]), ALU.mult).then_inc(msg_done, 1)
                        between((mean_step, 3, last_window), (out_step, 3, window_before))
                        if at + 2 < NG:
                            make_pick(r, k + 2, at + 2)
                        between((mean_step, 4, last_window), (out_step, 4, window_before),
                                (out_step, 5, window_before))
                        if at == NG - 1:
                            for n in range(MEAN_STEPS):
                                mean_step(n, *last_window)
                            for n in range(2):
                                out_step(n, *last_window)

                    for g in range(2):
                        make_pick(0, g, g)
                    make_place(0, 0, 0)
                    engine_turns(dve, arithmetic)

        def next_pass():
            nc.all_engine_barrier(sems_to_clear=range(sems[0].num, sems[-1].num + 1))

        def all_outputs():
            hsum = q_parts[:].rearrange("p t s d -> p (t s d)").bitcast(f32)[:, 0:OT * ML]
            hsum = hsum.rearrange("p (t f) -> p t f", t=OT)
            rows = kv[:].rearrange("p s t f -> p (s t f)")
            xr = rows[:, 0:OT * D].rearrange("p (t f) -> p t f", t=OT)
            y = xt[:, 0:OT * D].rearrange("p (t f) -> p t f", t=OT)
            y2 = rows[:, OT * D:2 * OT * D].rearrange("p (t f) -> p t f", t=OT)
            rzs = rows[:, 2 * OT * D:2 * OT * D + OT * H].rearrange("p (t h) -> p t h", t=OT)
            st = dst_stats
            with nc.Block() as block:
                @block.sync
                def _(sp):
                    sp.dma_start(hsum, acc_table[0:NW * P, :].rearrange("(p t) f -> p t f", p=P)).then_inc(w_in, 16)
                    sp.dma_start(xr, xrows[0:NW * P, :].rearrange("(p t) f -> p t f", p=P)).then_inc(we_in, 16)
                    sp.wait_ge(fin_done, 1)
                    sp.dma_start(out[0:NW * P, :].rearrange("(p t) f -> p t f", p=P), y).then_inc(kv_out, 16)
                    sp.wait_ge(kv_out, 16)

                @block.scalar
                def _(act):
                    act.wait_ge(log_done, 1)
                    nc.scalar.activation(y2, y, ACT.Square).then_inc(root_done, 1)
                    act.wait_ge(log_done, 2)
                    nc.scalar.activation(st[:, 3], st[:, 2], ACT.Sqrt).then_inc(root_done, 1)

                @block.vector
                def _(dve):
                    chained = [0]

                    def link(ins):
                        chained[0] += 1
                        ins.then_inc(tables_chain, 1)
                        dve.wait_ge(tables_chain, chained[0])

                    dve.wait_ge(w_in, 16)
                    link(nc.vector.tensor_scalar(rzs, hsum[:, :, D:ML], EPS_Z, None, ALU.add))
                    link(nc.vector.reciprocal(rzs, rzs))
                    link(nc.vector.tensor_tensor(y.rearrange("p t (h d) -> p t h d", h=H),
                                                 hsum[:, :, 0:D].rearrange("p t (h d) -> p t h d", h=H),
                                                 rzs.unsqueeze(3).broadcast_to([P, OT, H, HD]), ALU.mult))
                    dve.wait_ge(we_in, 16)
                    link(nc.vector.tensor_tensor(y, y, xr, ALU.add))
                    link(nc.vector.reduce_sum(st[:, 0], y, AX.X))
                    link(nc.vector.tensor_scalar(st[:, 1], st[:, 0], 1.0 / D, None, ALU.mult))
                    nc.vector.tensor_tensor(y, y, st[:, 1].unsqueeze(2).broadcast_to([P, OT, D]),
                                            ALU.subtract).then_inc(log_done, 1)
                    dve.wait_ge(root_done, 1)
                    link(nc.vector.reduce_sum(st[:, 0], y2, AX.X))
                    nc.vector.tensor_scalar(st[:, 2], st[:, 0], 1.0 / D, EPS_LN, ALU.mult, ALU.add
                                            ).then_inc(log_done, 1)
                    dve.wait_ge(root_done, 2)
                    link(nc.vector.reciprocal(st[:, 4], st[:, 3]))
                    nc.vector.tensor_tensor(y, y, st[:, 4].unsqueeze(2).broadcast_to([P, OT, D]),
                                            ALU.mult).then_inc(fin_done, 1)

        dst_stats = sb("dst_stats", [P, 5, OT], f32)
        edge_pass(True)
        left = nc.values_load(left_int[0:1, 0:1], min_val=0, max_val=2)
        with nc.If(left > 0):
            next_pass()
            with nc.If(left > 1):
                with nc.Fori(1, NW):
                    edge_pass(False)
                    next_pass()
            all_outputs()


def kernel(x, src, dst, edge_attr_96, L0_gnn_Wq, L0_gnn_bq, L0_gnn_Wk, L0_gnn_bk, L0_gnn_We, L0_gnn_be,
           L0_gnn_Wv, L0_gnn_bv):
    import numpy as np
    import concourse.bacc as bacc
    from concourse.bass_utils import run_bass_kernel_spmd

    x, src, dst, ea = (np.asarray(a) for a in (x, src, dst, edge_attr_96))
    wq, bq, wk, bk, we, be, wv, bv = (np.asarray(a) for a in (
        L0_gnn_Wq, L0_gnn_bq, L0_gnn_Wk, L0_gnn_bk, L0_gnn_We, L0_gnn_be, L0_gnn_Wv, L0_gnn_bv))
    xT = np.zeros((D, NR), x.dtype)
    xT[:, :N] = x.T
    xrows = np.zeros((NR, D), x.dtype)
    xrows[:N] = x
    src_pad = np.zeros(NG * GE, src.dtype)
    src_pad[:E] = src
    dst_pad = np.full(NG * GE, N, dst.dtype)
    dst_pad[:E] = dst
    eaT = np.zeros((NG * GE, D), ea.dtype)
    eaT[:E] = ea
    arrays = {
        "xT": xT,
        "ones": np.ones((1, NR), x.dtype),
        "xrows": xrows,
        "src": np.ascontiguousarray(src_pad.reshape(NG, T, P).transpose(0, 2, 1)),
        "dst_group": dst_pad.reshape(NG, GE),
        "dst_tile": np.ascontiguousarray(dst_pad.reshape(NG * T, P).T),
        "eaT": np.ascontiguousarray(eaT.reshape(NG, GE, D).transpose(0, 2, 1)),
        "w_node": np.concatenate([np.concatenate([wk, wv, wq], 1), np.concatenate([bk, bv, bq])[None]], 0),
        "w_edge": np.concatenate([we, be[None]], 0),
    }
    nc = bacc.Bacc("TRN2", target_bir_lowering=False, num_devices=1)
    args = [nc.dram_tensor(n, a.shape, mybir.dt.from_np(a.dtype), kind="ExternalInput").ap()
            for n, a in arrays.items()]
    out = nc.dram_tensor("out", (NR, D), mybir.dt.float32, kind="ExternalOutput").ap()
    gnn_program(nc, *args, out)
    r = run_bass_kernel_spmd(nc, [arrays], core_ids=[0])
    return r.results[0]["out"][:N]
```
